# Optimizing a Trainium2 kernel written in Bass

```python
import numpy as np
import jax
import jax.numpy as jnp

def _softmax(x, axis=-1):
    return jax.nn.softmax(x, axis=axis)

def _gelu(x):
    return jax.nn.gelu(x, approximate=True)

def _silu(x):
    return jax.nn.silu(x)

def _sigmoid(x):
    return jax.nn.sigmoid(x)

def _layernorm(x, axis=-1, eps=1e-05):
    m = jnp.mean(x, axis=axis, keepdims=True)
    v = jnp.var(x, axis=axis, keepdims=True)
    return (x - m) / jnp.sqrt(v + eps)

def _scatter_add(tgt, idx, src, axis=0):
    return tgt.at[idx].add(src)

def _segment_sum(src, seg, n):
    return jax.ops.segment_sum(src, seg, n)
kernel_name = 'mk_gnn_ffn_d1_gnn_r8_598445'

def setup_inputs(seed: int=0):
    np.random.seed(seed)
    _w = jnp.asarray

    def _rec_inputs():
        import jax
        import jax.numpy as jnp
        _gk = jax.random.key(seed)
        x = -0.0002117 + 1 * jax.random.normal(jax.random.fold_in(_gk, 1), (6250, 256), jnp.float32)
        _s = jax.random.randint(jax.random.fold_in(_gk, 2), (50000,), 0, 6250, jnp.int32)
        _d = jax.random.randint(jax.random.fold_in(_gk, 3), (50000,), 0, 6250, jnp.int32)
        _loop = jnp.arange(6250, dtype=jnp.int32)
        src = jnp.concatenate([_s, _d, _loop])
        dst = jnp.concatenate([_d, _s, _loop])
        _o = jnp.argsort(dst, stable=True)
        src = src[_o]
        dst = dst[_o]
        return (x, src, dst)
    x, src, dst = _rec_inputs()

    def _L0_gnn_setup():
        import jax, jax.numpy as jnp
        import numpy as np
        N_NODES = 12500
        CHANNELS = 256
        REDUCTION = 4
        K = 2
        N_EDGES = 400000

        def _gcn_conv(x, edge_index, W, b):
            N = x.shape[0]
            loop = jnp.arange(N, dtype=edge_index.dtype)
            src = jnp.concatenate([edge_index[0], loop])
            dst = jnp.concatenate([edge_index[1], loop])
            deg = jax.ops.segment_sum(jnp.ones_like(dst, dtype=x.dtype), dst, num_segments=N)
            dis = jnp.where(deg > 0, jax.lax.rsqrt(deg), 0.0)
            norm = dis[src] * dis[dst]
            h = x @ W
            agg = jax.ops.segment_sum(h[src] * norm[:, None], dst, num_segments=N)
            return agg + b
        key = jax.random.key(seed)
        k1, k2, k3, k4 = jax.random.split(key, 4)
        hid = CHANNELS // REDUCTION
        x = jax.random.normal(k1, (N_NODES, CHANNELS), dtype=jnp.float32)
        edge_index = jax.random.randint(k2, (2, N_EDGES), 0, N_NODES, dtype=jnp.int64)
        W1 = jax.random.normal(k3, (CHANNELS, hid), dtype=jnp.float32) / np.sqrt(CHANNELS)
        b1 = jnp.zeros((hid,), dtype=jnp.float32)
        W2 = jax.random.normal(k4, (hid, 2 * K * CHANNELS), dtype=jnp.float32) / np.sqrt(hid)
        b2 = jnp.zeros((2 * K * CHANNELS,), dtype=jnp.float32)
        return {'x': x, 'edge_index': edge_index, 'W1': W1, 'b1': b1, 'W2': W2, 'b2': b2}
    _L0_gnn_all = _L0_gnn_setup()
    _L0_gnn_in = {k: v for k, v in _L0_gnn_all.items() if k in ('W1', 'b1', 'W2', 'b2')}
    del _L0_gnn_all

    def _L0_ffn_setup():
        import jax, jax.numpy as jnp
        import numpy as np
        B, S, H, F, E, K = (8, 512, 256, 512, 16, 2)
        EPS = 1e-05
        key = jax.random.key(seed)
        ks = jax.random.split(key, 9)
        sc = 0.02
        return {'x': jax.random.normal(ks[0], (B, S, H), dtype=jnp.float32), 'gate_w': jax.random.normal(ks[1], (H, E), dtype=jnp.float32) * sc, 'gate_b': jnp.zeros((E,), dtype=jnp.float32), 'w1': jax.random.normal(ks[2], (E, H, F), dtype=jnp.float32) * sc, 'b1': jnp.zeros((E, F), dtype=jnp.float32), 'w2': jax.random.normal(ks[3], (E, F, H), dtype=jnp.float32) * sc, 'b2': jnp.zeros((E, H), dtype=jnp.float32), 'gamma': jnp.ones((H,), dtype=jnp.float32), 'beta': jnp.zeros((H,), dtype=jnp.float32)}
    _L0_ffn_all = _L0_ffn_setup()
    _L0_ffn_in = {k: v for k, v in _L0_ffn_all.items() if k in ('gate_w', 'gate_b', 'w1', 'b1', 'w2', 'b2', 'gamma', 'beta')}
    del _L0_ffn_all
    return {'x': x, 'src': src, 'dst': dst, 'L0_gnn_W1': _L0_gnn_in['W1'], 'L0_gnn_b1': _L0_gnn_in['b1'], 'L0_gnn_W2': _L0_gnn_in['W2'], 'L0_gnn_b2': _L0_gnn_in['b2'], 'L0_ffn_gate_w': _L0_ffn_in['gate_w'], 'L0_ffn_gate_b': _L0_ffn_in['gate_b'], 'L0_ffn_w1': _L0_ffn_in['w1'], 'L0_ffn_b1': _L0_ffn_in['b1'], 'L0_ffn_w2': _L0_ffn_in['w2'], 'L0_ffn_b2': _L0_ffn_in['b2'], 'L0_ffn_gamma': _L0_ffn_in['gamma'], 'L0_ffn_beta': _L0_ffn_in['beta']}

def reference(x, src, dst, L0_gnn_W1, L0_gnn_b1, L0_gnn_W2, L0_gnn_b2, L0_ffn_gate_w, L0_ffn_gate_b, L0_ffn_w1, L0_ffn_b1, L0_ffn_w2, L0_ffn_b2, L0_ffn_gamma, L0_ffn_beta):
    import jax
    import jax.numpy as jnp

    def _L0_gnn_ref(x, edge_index, W1, b1, W2, b2):
        import jax, jax.numpy as jnp
        import numpy as np
        N_NODES = 12500
        CHANNELS = 256
        REDUCTION = 4
        K = 2
        N_EDGES = 400000

        def _gcn_conv(x, edge_index, W, b):
            N = x.shape[0]
            loop = jnp.arange(N, dtype=edge_index.dtype)
            src = jnp.concatenate([edge_index[0], loop])
            dst = jnp.concatenate([edge_index[1], loop])
            deg = jax.ops.segment_sum(jnp.ones_like(dst, dtype=x.dtype), dst, num_segments=N)
            dis = jnp.where(deg > 0, jax.lax.rsqrt(deg), 0.0)
            norm = dis[src] * dis[dst]
            h = x @ W
            agg = jax.ops.segment_sum(h[src] * norm[:, None], dst, num_segments=N)
            return agg + b
        k = K
        C = x.shape[1]
        theta = _gcn_conv(x, edge_index, W1, b1)
        theta = jax.nn.relu(jnp.mean(theta, axis=0))
        theta = theta @ W2 + b2
        theta = 2.0 * jax.nn.sigmoid(theta) - 1.0
        lambdas = jnp.array([1.0] * k + [0.5] * k, dtype=x.dtype)
        init_v = jnp.array([1.0] + [0.0] * (2 * k - 1), dtype=x.dtype)
        coefs = theta.reshape(C, 2 * k) * lambdas + init_v
        out = x[:, :, None] * coefs[None, :, :k] + coefs[None, :, k:]
        return jnp.max(out, axis=-1)

    def _L0_ffn_ref(x, gate_w, gate_b, w1, b1, w2, b2, gamma, beta):
        import jax, jax.numpy as jnp
        import numpy as np
        B, S, H, F, E, K = (8, 512, 256, 512, 16, 2)
        EPS = 1e-05
        gate_logits = x @ gate_w + gate_b
        topk_vals, topk_idx = jax.lax.top_k(gate_logits, K)
        topk_w = jax.nn.softmax(topk_vals, axis=-1)
        h = jax.nn.relu(jnp.einsum('bsh,ehf->bsef', x, w1) + b1)
        expert_out = jnp.einsum('bsef,efh->bseh', h, w2) + b2
        sel = jnp.take_along_axis(expert_out, topk_idx[:, :, :, None], axis=2)
        moe = jnp.sum(topk_w[..., None] * sel, axis=2)
        y = x + moe
        mu = jnp.mean(y, axis=-1, keepdims=True)
        var = jnp.var(y, axis=-1, keepdims=True)
        return (y - mu) / jnp.sqrt(var + EPS) * gamma + beta
    edge_index = jnp.stack([src, dst])
    x = x + _L0_gnn_ref(_layernorm(x, axis=-1), edge_index, L0_gnn_W1, L0_gnn_b1, L0_gnn_W2, L0_gnn_b2)
    x = x + _L0_ffn_ref(_layernorm(x, axis=-1)[None], L0_ffn_gate_w, L0_ffn_gate_b, L0_ffn_w1, L0_ffn_b1, L0_ffn_w2, L0_ffn_b2, L0_ffn_gamma, L0_ffn_beta)[0]
    return x

_drawn_inputs = setup_inputs


def setup_inputs(seed=0):
    import zlib

    import numpy as np

    out = dict(_drawn_inputs(seed))
    spreads = {'L0_gnn_b1': (0.0, 0.325),
     'L0_gnn_b2': (0.0, 0.1),
     'L0_ffn_gate_b': (0.0, 0.297),
     'L0_ffn_b1': (0.0, 0.8),
     'L0_ffn_b2': (0.0, 0.279),
     'L0_ffn_gamma': (1.0, 0.2),
     'L0_ffn_beta': (0.0, 0.1)}
    factors = {'L0_gnn_W1': 8.0}
    for name, (base, spread) in spreads.items():
        noise = np.random.default_rng([zlib.crc32(name.encode()), seed]).standard_normal(out[name].shape)
        drawn = base * np.exp(spread * noise) if base else spread * noise
        out[name] = jnp.asarray(drawn.astype(out[name].dtype))
    for name, factor in factors.items():
        out[name] = (out[name] * factor).astype(out[name].dtype)
    return out
```

```python
import concourse.bass as bass
from concourse import mybir
from contextlib import ExitStack

P = 128
N, C = 6250, 256
EDGES = 106250
HID = 64
E, F = 16, 512
NT = -(-N // P)
LAST = N - (NT - 1) * P
EPS = 1e-5

EC = EDGES // P
ETAIL = EDGES - EC * P
GC = 32
NCH = 832
NG = NCH // GC
PAD_INDEX = 8191
LO_BITS = 7
BLK = -(-NCH // P)

GT = 7
NGT = NT // GT

CAP = 6400
MT = 114
XROWS = E * CAP
WCOLS = 2 * C * F // P
assert MT * P >= 2 * N + E * (P - 1) and MT % 2 == 0 and N + P <= CAP
assert NG * GC == NCH and NG % 2 == 0 and NGT * GT == NT and NGT % 2 == 1


def build(nc, x, src, dst, gW1, gb1, gW2, gb2, gate_w, gate_b, w1, b1, w2, b2, gamma, beta, out):
    fp32, bf16, fp16 = mybir.dt.float32, mybir.dt.bfloat16, mybir.dt.float16
    i32, u32 = mybir.dt.int32, mybir.dt.uint32
    ALU = mybir.AluOpType
    ACT = mybir.ActivationFunctionType
    AX = mybir.AxisListType
    ds = bass.ds

    ctx = ExitStack()
    with ctx:
        def sb(name, shape, dt):
            return ctx.enter_context(nc.sbuf_tensor(name, shape, dt))

        def sem(name):
            return ctx.enter_context(nc.semaphore(name))

        lo_rows = nc.dram_tensor("lo_rows", (NCH, P), bf16, kind="Internal").ap()
        xs = nc.dram_tensor("xs", (XROWS, C), fp32, kind="Internal").ap()
        ys = nc.dram_tensor("ys", (MT * P, C), fp32, kind="Internal").ap()

        W = sb("W", [P, E * WCOLS], fp32)
        XH = sb("XH", [P, NT, C], fp32)
        RB = 14336
        R = sb("R", [P, RB // 4], fp32)

        def carve(base, start):
            at = [start]

            def take(dims, dt):
                size = {fp32: 4, i32: 4, u32: 4, bf16: 2, fp16: 2}[dt]
                n = size
                for d in dims:
                    n *= d
                n = -(-n // 4) * 4
                v = base[:, at[0] // 4:(at[0] + n) // 4]
                if dt != fp32:
                    v = v.bitcast(dt)
                at[0] += n
                if len(dims) == 2:
                    v = v.rearrange("p (a b) -> p a b", a=dims[0])
                elif len(dims) == 3:
                    v = v.rearrange("p (a b c) -> p a b c", a=dims[0], b=dims[1])
                elif len(dims) == 4:
                    v = v.rearrange("p (a b c d) -> p a b c d", a=dims[0], b=dims[1], c=dims[2])
                return v
            return take, at

        EARLY = 4
        MIDDLE = 9
        take, at = carve(W, EARLY * WCOLS * 4)
        iota_lo = take([P, GC], bf16)
        iota_hi = take([NT, GC], bf16)
        oh_lo = take([2, P, GC], bf16)
        oh_hi = take([2, NT, GC], bf16)
        oh_src = take([2, NT, GC], bf16)
        ints = at[0]
        oh_t = take([2, GC * P], bf16)
        lo_bc = take([2, GC * P], bf16)
        picked = take([GC, NT], fp32)
        weighted = take([2, 2, NT, GC], fp16)
        assert at[0] <= E * WCOLS * 4
        take, at = carve(W, ints)
        dst_i = take([NCH], i32)
        src_i = take([NCH], i32)
        hi_i = take([NCH], i32)
        lo_i = take([NCH], i32)
        take, at = carve(R, 0)
        dlo = take([NCH], bf16)
        dhi = take([NCH], bf16)
        slo = take([NCH], bf16)
        shi = take([NCH], bf16)
        loT = take([BLK, P], bf16)
        junk = take([C], fp32)
        g_val = take([GC], fp32)
        g_rest = take([GC], fp32)
        g_two = take([2, GC], fp16)
        gW1_sb = take([2, HID], fp32)
        th_bc = take([P], fp32)
        lnsum = take([NT], fp32)
        lnsq = take([NT], fp32)
        nmean = take([NT], fp32)
        deg = take([NT], fp32)
        assert at[0] <= RB
        take, at = carve(W, EARLY * WCOLS * 4)
        gb2_bc = take([4 * C], fp32)
        theta = take([4 * C], fp32)
        gW2_sb = take([4 * C], fp32)
        take, at = carve(W, MIDDLE * WCOLS * 4)
        x_in = take([2, GT, C], fp32)
        branch = take([GT, C], fp32)
        xn = take([2, GT, C], fp32)
        xnT = take([GT, 2, P], fp32)
        assert at[0] <= E * WCOLS * 4
        take, at = carve(R, 0)
        zrows = take([C], fp32)
        coef = take([4, C], fp32)
        assert at[0] <= RB
        take, at = carve(R, 0)
        X3 = take([2, C], fp32)
        XT3 = take([2, 2, P], fp32)
        H3 = take([2, F], fp32)
        HT3 = take([2, 4, P], fp32)
        O3 = take([2, C], fp32)
        assert at[0] <= RB
        take, at = carve(W, 0)
        pick0 = take([2, C], fp32)
        pick1 = take([2, C], fp32)
        xn4 = take([2, C], fp32)
        acc4 = take([2, C], fp32)
        y4 = take([2, C], fp32)
        x1b4 = take([2, C], fp32)
        out4 = take([2, C], fp32)
        gm_s = take([2, E], fp32)
        gmT = take([2, P], fp32)
        gamma_bc = take([C], fp32)
        beta_bc = take([C], fp32)
        st4 = take([2, 6], fp32)
        mv4 = take([2, 2], fp32)
        ve4 = take([2, 1], fp32)
        sd4 = take([2, 1], fp32)
        rs4 = take([2, 1], fp32)
        nm4 = take([2, 1], fp32)

        ident = sb("ident", [P, P], fp32)
        identb = sb("identb", [P, P], bf16)
        upper = sb("upper", [P, P], bf16)
        onesb = sb("onesb", [P, P], bf16)
        zerob = sb("zerob", [P, P], bf16)
        iota_p = sb("iota_p", [P, 1], fp32)
        iota16 = sb("iota16", [P, E], fp32)
        rowmask = sb("rowmask", [P, 1], fp32)
        gw_sb = sb("gw_sb", [P, 2, E], fp32)
        gateb_bc = sb("gateb_bc", [P, E], fp32)
        gb1_col = sb("gb1_col", [HID, 1], fp32)
        b1T = sb("b1T", [P, E, 4], fp32)
        b2_sb = sb("b2_sb", [E, C], fp32)
        nmr = sb("nmr", [P, NT], fp32)
        rstd = sb("rstd", [P, NT], fp32)
        sd = sb("sd", [P, NT], fp32)
        dis = sb("dis", [P, NT], fp32)
        tmpa = sb("tmpa", [P, NT], fp32)
        tmpb = sb("tmpb", [P, NT], fp32)
        dis3 = sb("dis3", [P, 3, NT], bf16)
        wts = sb("wts", [P, NT], fp32)
        vcol = sb("vcol", [P, 2], fp32)
        th = sb("th", [HID, 1], fp32)
        mv2 = sb("mv2", [P, GT, 2], fp32)
        st2 = sb("st2", [P, GT, 6], fp32)
        logit = sb("logit", [P, GT, E], fp32)
        top = sb("top", [P, GT, 8], fp32)
        topi = sb("topi", [P, GT, 8], u32)
        IDX = sb("IDX", [P, NT, 2], fp32)
        TOPV = sb("TOPV", [P, NT, 2], fp32)
        SLOT = sb("SLOT", [P, NT, 2], fp32)
        WT = sb("WT", [P, 2, NT], fp32)
        oh = sb("oh", [P, 2, GT, E], fp32)
        cnt_in = sb("cnt_in", [P, GT + 1, E], bf16)
        posq = sb("posq", [P, GT, E], fp32)
        prodq = sb("prodq", [P, GT, E], fp32)
        carry = sb("carry", [P, E], fp32)
        ecap = sb("ecap", [P, E], fp32)
        slot_i = sb("slot_i", [P, 2, GT, 2], i32)
        pad_i = sb("pad_i", [1, E], i32)
        cnti = sb("cnti", [P, E], i32)
        nt16 = sb("nt16", [P, E], fp32)
        cum = sb("cum", [P, 2, E], fp32)
        fin16 = sb("fin16", [P, E], fp32)
        p16 = sb("p16", [P, E], fp32)
        et = sb("et", [P, 4], fp32)
        tile_e = sb("tile_e", [1, P], i32)
        tile_r = sb("tile_r", [1, P], i32)
        dbase = sb("dbase", [P, E], fp32)
        GM = sb("GM", [P, NT, E], fp32)
        SLOTI = sb("SLOTI", [P, NT, 2], i32)
        gidx = sb("gidx", [P, 4], i32)

        PS = ctx.enter_context(nc.psum_tensor("PS", [P, 8, 512], fp32))

        def wt1(e_col, k):
            return W[:, ds(e_col + k * F, F)]

        def wt2(e_col, j):
            return W[:, ds(e_col + 2 * F + j * C, C)]

        def load_expert(eng, e, done):
            eng.dma_start(W[:, e * WCOLS:e * WCOLS + 2 * F],
                          w1[e].rearrange("(p k) f -> p (k f)", k=2)).then_inc(done, 16)
            eng.dma_start(W[:, e * WCOLS + 2 * F:(e + 1) * WCOLS],
                          w2[e].rearrange("(p j) h -> p (j h)", j=4)).then_inc(done, 16)

        weights_in = sem("weights_in")
        pool_mark = sem("pool_mark")

        def linker(eng, signal, start=0):
            state = [start, 0]

            def link(ins):
                state[1] += 1
                ins.then_inc(signal, 1)
                eng.wait_ge(signal, state[0] + state[1])

            def rebase(base):
                state[0], state[1] = base, 0
            link.rebase = rebase
            link.state = state
            return link

        def wait_past(eng, signal, count):
            if not isinstance(count, int) or count > 0:
                eng.wait_ge(signal, count)

        consts_set = sem("consts_set")
        pads_set = sem("pads_set")
        idx_in = sem("idx_in")
        x_loaded = sem("x_loaded")
        small_in = sem("small_in")
        gb2_in = sem("gb2_in")
        dve_step = sem("dve_step")
        act_step = sem("act_step")
        idx_split = sem("idx_split")
        lo_turned = sem("lo_turned")
        loT_copied = sem("loT_copied")
        lo_stored = sem("lo_stored")
        lo_bc_in = [sem("lo_bc_in0"), sem("lo_bc_in1")]
        deg_onehots = sem("deg_onehots")
        deg_free = sem("deg_free")
        deg_done = sem("deg_done")
        deg_ready = sem("deg_ready")
        deg_rooted = sem("deg_rooted")
        dis_ready = sem("dis_ready")
        oht_ready = sem("oht_ready")
        looked_up = sem("looked_up")
        lookup_free = sem("lookup_free")
        src_free = sem("src_free")
        deg_lo = sem("deg_lo")
        weighted_ready = sem("weighted_ready")
        sums_done = sem("sums_done")
        mean_ready = sem("mean_ready")
        sq_done = sem("sq_done")
        var_ready = sem("var_ready")
        sd_ready = sem("sd_ready")
        norm_ready = sem("norm_ready")
        xhat_ready = sem("xhat_ready")
        node_w = sem("node_w")
        v_done = sem("v_done")
        v_copied = sem("v_copied")
        th_done = sem("th_done")
        th_bcast = sem("th_bcast")
        z_done = sem("z_done")
        z_ready = sem("z_ready")
        sig_ready = sem("sig_ready")

        S1_DEG = 0
        S1_ACC = 1

        N_CONSTS = 16

        with nc.Block() as block:
            @block.gpsimd
            def _(pool):
                pool.memset(XH[96:P, NT - 1, :], 0.0).then_inc(pads_set, 1)
                pool.wait_ge(pads_set, 1)
                pool.memset(dst_i[:, EC:NCH], PAD_INDEX).then_inc(pads_set, 1)
                pool.memset(src_i[:, EC:NCH], PAD_INDEX).then_inc(pads_set, 1)
                made = [0]

                def const(ins):
                    ins.then_inc(consts_set, 1)
                    made[0] += 1

                const(pool.iota(iota_lo, pattern=[[1, P], [0, GC]], base=0, channel_multiplier=0,
                                allow_small_or_imprecise_dtypes=True))
                const(pool.iota(iota_hi, pattern=[[1, NT], [0, GC]], base=0, channel_multiplier=0,
                                allow_small_or_imprecise_dtypes=True))
                const(pool.memset(ident[:, :], 0.0))
                const(pool.memset(identb[:, :], 0.0))
                const(pool.memset(upper[:, :], 1.0))
                const(pool.memset(onesb[:, :], 1.0))
                const(pool.memset(zerob[:, :], 0.0))
                const(pool.memset(rowmask[:, :], 1.0))
                const(pool.memset(cnt_in[:, :, :], 0.0))
                const(pool.iota(iota_p[:, :], pattern=[[0, 1]], base=0, channel_multiplier=1,
                                allow_small_or_imprecise_dtypes=True))
                const(pool.iota(iota16[:, :], pattern=[[1, E]], base=0, channel_multiplier=0,
                                allow_small_or_imprecise_dtypes=True))
                const(pool.iota(ecap[:, :], pattern=[[CAP, E]], base=0, channel_multiplier=0,
                                allow_small_or_imprecise_dtypes=True))
                pool.wait_ge(consts_set, made[0])
                for m in (ident, identb):
                    const(pool.affine_select(out=m[:, :], in_=m[:, :], compare_op=ALU.not_equal, fill=1.0,
                                             base=0, pattern=[[-1, P]], channel_multiplier=1))
                const(pool.affine_select(out=upper[:, :], in_=upper[:, :], compare_op=ALU.is_gt, fill=0.0,
                                         base=0, pattern=[[1, P]], channel_multiplier=-1))
                const(pool.affine_select(out=rowmask[:, :], in_=rowmask[:, :], compare_op=ALU.is_gt, fill=0.0,
                                         base=LAST, pattern=[[0, 1]], channel_multiplier=-1))
                assert made[0] == N_CONSTS

            @block.sync
            def _(sp):
                sp.wait_ge(pads_set, 3)
                for a, b in ((dst, dst_i), (src, src_i)):
                    sp.dma_start(b[:, 0:EC], a[0:EC * P].rearrange("(p c) -> p c", p=P)).then_inc(idx_in, 16)
                    sp.dma_start(b[0:ETAIL, EC:EC + 1],
                                 a[EC * P:EDGES].rearrange("(p c) -> p c", p=ETAIL)).then_inc(idx_in, 16)
                sp.dma_start(XH[:, 0:NT - 1, :],
                             x[0:(NT - 1) * P, :].rearrange("(t p) c -> p t c", p=P)).then_inc(x_loaded, 16)
                sp.dma_start(XH[0:LAST, NT - 1, :], x[(NT - 1) * P:N, :]).then_inc(x_loaded, 16)
                for e in range(EARLY):
                    load_expert(sp, e, weights_in)
                sp.wait_ge(loT_copied, 2)
                sp.dma_start(lo_rows[0:(BLK - 1) * P, :].rearrange("(b q) m -> q b m", q=P),
                             loT[:, 0:BLK - 1, :]).then_inc(lo_stored, 16)
                sp.dma_start(lo_rows[(BLK - 1) * P:NCH, :],
                             loT[0:NCH - (BLK - 1) * P, BLK - 1, :]).then_inc(lo_stored, 16)
                sp.wait_ge(lo_stored, 32)

                def load_lo(g, u):
                    sp.dma_start(lo_bc[:, u, :],
                                 lo_rows[ds(g * GC, GC), :].rearrange("c m -> (c m)").partition_broadcast(P)
                                 ).then_inc(lo_bc_in[u], 16)
                sp.wait_ge(idx_split, 4)
                load_lo(0, 0)
                load_lo(1, 1)
                with sp.Fori(1, NG // 2) as i:
                    for u in range(2):
                        sp.wait_ge(oht_ready, 2 * i + (u - 1))
                        load_lo(2 * i + u, u)
                sp.wait_ge(src_free, NG + 2)
                sp.dma_start(gW2_sb[0:HID, :], gW2).then_inc(gb2_in, 16)
                sp.dma_start(gb2_bc, gb2.partition_broadcast(P)).then_inc(gb2_in, 16)

            @block.scalar
            def _(act):
                act.dma_start(gw_sb[:, :, :], gate_w.rearrange("(p k) e -> p k e", k=2)).then_inc(small_in, 16)
                act.dma_start(gateb_bc[:, :], gate_b.partition_broadcast(P)).then_inc(small_in, 16)
                act.dma_start(gW1_sb[:, :, :], gW1.rearrange("(k p) h -> p k h", p=P)).then_inc(small_in, 16)
                act.dma_start(gb1_col[:, :], gb1.rearrange("(p o) -> p o", o=1)).then_inc(small_in, 16)
                act.dma_start(b1T[:, :, :], b1.rearrange("e (p j) -> p e j", j=4)).then_inc(small_in, 16)
                act.dma_start(b2_sb[:, :], b2).then_inc(small_in, 16)
                act.wait_ge(lo_turned, 1)
                turned = PS[:, 2, :].bitcast(bf16).rearrange("p (b m) -> p b m", m=P)
                act.activation(loT[:, 0:BLK - 1, :], turned[:, 0:BLK - 1, :], ACT.Copy).then_inc(loT_copied, 1)
                act.activation(loT[0:64, BLK - 1, :], turned[0:64, BLK - 1, :], ACT.Copy).then_inc(loT_copied, 1)
                act.wait_ge(x_loaded, 32)
                link = linker(act, act_step)
                with act.Fori(0, NT) as t:
                    link.rebase(t)
                    link(nc.scalar.activation(junk, XH[:, ds(t, 1), :].rearrange("p o c -> p (o c)"), ACT.Copy,
                                              accum_out=lnsum[:, ds(t, 1)]))
                act.activation(sd[:, :], lnsum, ACT.Copy).then_inc(sums_done, 1)
                act.wait_ge(deg_ready, 1)
                act.activation(tmpa[:, :], deg[:, :], ACT.Sqrt).then_inc(deg_rooted, 1)
                act.wait_ge(mean_ready, 1)
                with act.Fori(0, NT) as t:
                    link.rebase(t + NT)
                    link(nc.scalar.activation(junk, XH[:, ds(t, 1), :].rearrange("p o c -> p (o c)"), ACT.Square,
                                              bias=nmean[:, ds(t, 1)], accum_out=lnsq[:, ds(t, 1)]))
                act.activation(sd[:, :], lnsq, ACT.Copy).then_inc(sq_done, 1)
                act.wait_ge(var_ready, 1)
                act.activation(sd[:, :], lnsq[:, :], ACT.Sqrt).then_inc(sd_ready, 1)
                act.wait_ge(norm_ready, 1)
                with act.Fori(0, NT) as t:
                    row = XH[:, ds(t, 1), :].rearrange("p o c -> p (o c)")
                    nc.scalar.activation(row, row, ACT.Identity, bias=nmr[:, ds(t, 1)],
                                         scale=rstd[:, ds(t, 1)]).then_inc(xhat_ready, 1)
                act.wait_ge(v_done, 1)
                act.activation(vcol[:, :], PS[:, 2, 0:2], ACT.Copy).then_inc(v_copied, 1)
                act.wait_ge(th_done, 1)
                act.wait_ge(small_in, 96)
                act.activation(th[:, :], PS[0:HID, 3, 0:1], ACT.Relu, bias=gb1_col[:, :],
                               scale=1.0 / N).then_inc(th_bcast, 1)
                act.wait_ge(th_bcast, 1)
                act.activation(th_bc[0:HID, :], th[:, :].to_broadcast([HID, P]), ACT.Copy).then_inc(th_bcast, 1)
                act.wait_ge(z_ready, 1)
                act.activation(theta, gb2_bc, ACT.Sigmoid).then_inc(sig_ready, 1)

            @block.tensor
            def _(pe):
                pe.wait_ge(consts_set, N_CONSTS)
                pe.wait_ge(idx_split, 1)
                turned = PS[:, 2, :].bitcast(bf16).rearrange("p (b m) -> p b m", m=P)
                for b in range(BLK):
                    cols = min(P, NCH - b * P)
                    last = nc.tensor.transpose(turned[0:cols, b, :], dlo[:, b * P:b * P + cols], identb[:, :])
                last.then_inc(lo_turned, 1)
                nc.tensor.matmul(PS[:, S1_DEG, 0:NT], zerob[:, :], zerob[:, 0:NT], start=True, stop=False)
                pe.sem_inc(deg_free, 2)
                with pe.Fori(0, NG // 2) as i:
                    for u in range(2):
                        pe.wait_ge(deg_onehots, 2 * i + (u + 1))
                        for c in range(GC):
                            last = nc.tensor.matmul(PS[:, S1_DEG, 0:NT], oh_lo[:, u, :, c], oh_hi[:, u, :, c],
                                                    start=False, stop=False)
                        last.then_inc(deg_free, 1)
                nc.tensor.matmul(PS[:, S1_DEG, 0:NT], zerob[:, :], zerob[:, 0:NT], start=False,
                                 stop=True).then_inc(deg_done, 1)
                nc.tensor.matmul(PS[:, S1_ACC, 0:2 * NT], zerob[:, :], zerob[:, 0:2 * NT], start=True, stop=False)
                pe.wait_ge(dis_ready, 1)
                pe.wait_ge(loT_copied, 2)
                HC = GC // 2

                def lookup(g, u):
                    pe.wait_ge(oht_ready, g + 1)
                    for h in range(2):
                        pe.wait_ge(lookup_free, 2 * g + (h + 1))
                        for c in range(HC):
                            o = PS[:, 2 + 2 * h + c // 8, (c % 8) * NT:(c % 8 + 1) * NT]
                            lhs = oh_t[:, u, (h * HC + c) * P:(h * HC + c + 1) * P]
                            for k in range(3):
                                last = nc.tensor.matmul(o, lhs, dis3[:, k, :], start=(k == 0), stop=(k == 2))
                        last.then_inc(looked_up, 1)

                def scatter(g, u):
                    pe.wait_ge(weighted_ready, g + 1)
                    for c in range(GC):
                        last = nc.tensor.matmul(PS[:, S1_ACC, 0:2 * NT], oh_lo[:, u, :, c],
                                                weighted[:, u, :, :, c], start=False, stop=False)
                    last.then_inc(src_free, 1)

                with pe.Fori(0, NG // 2) as i:
                    for u in range(2):
                        lookup(2 * i + u, u)
                        scatter(2 * i + u, u)
                nc.tensor.matmul(PS[:, S1_ACC, 0:2 * NT], zerob[:, :], zerob[:, 0:2 * NT], start=False,
                                 stop=True).then_inc(deg_done, 1)
                pe.wait_ge(node_w, 1)
                pe.wait_ge(xhat_ready, NT)
                for k in range(2):
                    for t in range(NT):
                        last = nc.tensor.matmul(PS[:, 2, k:k + 1], XH[:, t, k * P:(k + 1) * P], wts[:, t:t + 1],
                                                start=(t == 0), stop=(t == NT - 1))
                last.then_inc(v_done, 1)
                pe.wait_ge(v_copied, 1)
                pe.wait_ge(small_in, 96)
                for k in range(2):
                    last = nc.tensor.matmul(PS[0:HID, 3, 0:1], gW1_sb[:, k, :], vcol[:, k:k + 1],
                                            start=(k == 0), stop=(k == 1))
                last.then_inc(th_done, 1)
                pe.wait_ge(th_bcast, 2)
                pe.wait_ge(gb2_in, 32)
                for q in range(2):
                    last = nc.tensor.matmul(PS[:, 4 + q, :], th_bc[0:HID, :], gW2_sb[0:HID, q * 512:(q + 1) * 512],
                                            start=True, stop=True)
                last.then_inc(z_done, 1)

            @block.vector
            def _(dve):
                link = linker(dve, dve_step)
                dve.wait_ge(idx_in, 64)
                dve.wait_ge(consts_set, N_CONSTS)
                for raw, lo, hi in ((dst_i, dlo, dhi), (src_i, slo, shi)):
                    if raw is src_i:
                        dve.wait_ge(idx_split, 2)
                    link(nc.vector.tensor_scalar(lo_i, raw, P - 1, None, ALU.bitwise_and))
                    nc.vector.tensor_copy(lo, lo_i).then_inc(idx_split, 1)
                    link(nc.vector.tensor_scalar(hi_i, raw, LO_BITS, None, ALU.logical_shift_right))
                    nc.vector.tensor_copy(hi, hi_i).then_inc(idx_split, 1)
                dve.wait_ge(idx_split, 4)

                def onehot(into, part, values, g, size):
                    return nc.vector.tensor_tensor(into, part[:, ds(g * GC, GC)].unsqueeze(1)
                                                   .to_broadcast([P, size, GC]), values, ALU.is_equal)

                with dve.Fori(0, NG // 2) as i:
                    for u in range(2):
                        g = 2 * i + u
                        dve.wait_ge(deg_free, g + 1)
                        onehot(oh_lo[:, u], dlo, iota_lo, g, P).then_inc(deg_lo, 1)
                        onehot(oh_hi[:, u], dhi, iota_hi, g, NT).then_inc(deg_onehots, 1)
                dve.wait_ge(sums_done, 1)
                nc.vector.tensor_scalar(nmean[:, :], lnsum[:, :], -1.0 / C, None, ALU.mult).then_inc(mean_ready, 1)
                dve.wait_ge(deg_done, 1)
                nc.vector.tensor_scalar(deg[:, :], PS[:, S1_DEG, 0:NT], 1.0, None, ALU.add).then_inc(deg_ready, 1)
                dve.wait_ge(deg_rooted, 1)
                link(nc.vector.reciprocal(dis[:, :], tmpa[:, :]))
                link(nc.vector.tensor_tensor(tmpb[:, :], dis[:, :], dis[:, :], ALU.mult))
                link(nc.vector.tensor_tensor(tmpb[:, :], tmpb[:, :], deg[:, :], ALU.mult))
                link(nc.vector.tensor_scalar(tmpb[:, :], tmpb[:, :], -0.5, 1.5, ALU.mult, ALU.add))
                link(nc.vector.tensor_tensor(dis[:, :], dis[:, :], tmpb[:, :], ALU.mult))
                link(nc.vector.tensor_copy(dis3[:, 0, :], dis[:, :]))
                link(nc.vector.tensor_tensor(tmpa[:, :], dis[:, :], dis3[:, 0, :], ALU.subtract))
                link(nc.vector.tensor_copy(dis3[:, 1, :], tmpa[:, :]))
                link(nc.vector.tensor_tensor(tmpb[:, :], tmpa[:, :], dis3[:, 1, :], ALU.subtract))
                nc.vector.tensor_copy(dis3[:, 2, :], tmpb[:, :]).then_inc(dis_ready, 1)
                dve.wait_ge(deg_free, NG + 2)
                dve.sem_inc(lookup_free, 2)
                dve.sem_inc(src_free, 2)
                before = link.state[1]
                PER = 2 * 12
                def lookup_pair(i, base):
                    link.rebase(i * PER + base)
                    for u in range(2):
                        g = 2 * i + u
                        dve.wait_ge(lo_bc_in[u], 16 * i + 16)
                        dve.wait_ge(src_free, g + 1)
                        nc.vector.tensor_scalar(oh_t[:, u, :], lo_bc[:, u, :], iota_p[:, :], None,
                                                ALU.is_equal).then_inc(oht_ready, 1)
                        link(onehot(oh_hi[:, u], dhi, iota_hi, g, NT))
                        link(onehot(oh_lo[:, u], slo, iota_lo, g, P))
                        link(onehot(oh_src[:, u], shi, iota_hi, g, NT))
                        for h in range(2):
                            dve.wait_ge(looked_up, 2 * g + (h + 1))
                            rows = PS[:, 2 + 2 * h:4 + 2 * h, 0:8 * NT]
                            hot = oh_hi[:, u].rearrange("p t c -> p c t")[:, h * (GC // 2):(h + 1) * (GC // 2), :]
                            for q in range(2):
                                ins = nc.vector.tensor_tensor(
                                    picked[:, h * 16 + q * 8:h * 16 + q * 8 + 8, :],
                                    PS[:, 2 + 2 * h + q, 0:8 * NT].rearrange("p (c t) -> p c t", t=NT),
                                    hot[:, q * 8:q * 8 + 8, :], ALU.mult)
                                link(ins)
                            dve.sem_inc(lookup_free, 1)
                        link(nc.vector.tensor_reduce(g_val, picked, AX.X, ALU.add))
                        link(nc.vector.tensor_copy(g_two[:, 0, :], g_val))
                        link(nc.vector.tensor_tensor(g_rest, g_val, g_two[:, 0, :], ALU.subtract))
                        link(nc.vector.tensor_scalar(g_two[:, 1, :], g_rest, 2048.0, None, ALU.mult))
                        for k in range(2):
                            ins = nc.vector.tensor_tensor(weighted[:, u, k], oh_src[:, u],
                                                          g_two[:, k, :].unsqueeze(1).to_broadcast([P, NT, GC]),
                                                          ALU.mult)
                            if k == 0:
                                link(ins)
                            else:
                                ins.then_inc(weighted_ready, 1)
                    assert link.state[1] == PER, link.state

                HALF = NG // 4
                with dve.Fori(0, HALF) as i:
                    lookup_pair(i, before)
                link.rebase(before + PER * HALF)
                dve.wait_ge(sq_done, 1)
                nc.vector.tensor_scalar(lnsq[:, :], lnsq[:, :], 1.0 / C, EPS, ALU.mult, ALU.add).then_inc(var_ready, 1)
                dve.wait_ge(sd_ready, 1)
                link(nc.vector.reciprocal(rstd[:, :], sd[:, :]))
                dve.wait_ge(mean_ready, 1)
                nc.vector.tensor_tensor(nmr[:, :], nmean[:, :], rstd[:, :], ALU.mult).then_inc(norm_ready, 1)
                with dve.Fori(HALF, NG // 2) as i:
                    lookup_pair(i, before + 1)
                before += 1
                dve.wait_ge(deg_done, 2)
                link.rebase(before + PER * (NG // 2))
                link(nc.vector.tensor_scalar(tmpa[:, :], PS[:, S1_ACC, NT:2 * NT], 1.0 / 2048, None, ALU.mult))
                link(nc.vector.tensor_tensor(tmpa[:, :], PS[:, S1_ACC, 0:NT], tmpa[:, :], ALU.add))
                link(nc.vector.tensor_tensor(tmpa[:, :], tmpa[:, :], dis[:, :], ALU.add))
                nc.vector.tensor_tensor(wts[:, :], tmpa[:, :], dis[:, :], ALU.mult).then_inc(node_w, 1)
                dve.wait_ge(z_done, 1)
                for q in range(2):
                    ins = nc.vector.tensor_tensor(gb2_bc[:, q * 512:(q + 1) * 512], PS[:, 4 + q, :],
                                                  gb2_bc[:, q * 512:(q + 1) * 512], ALU.add)
                    link(ins)
                dve.sem_inc(z_ready, 1)
                dve.wait_ge(sig_ready, 1)
                link(nc.vector.tensor_scalar(theta, theta, 2.0, -1.0, ALU.mult, ALU.add))
                th4 = theta.rearrange("p (c j) -> p j c", j=4)
                link(nc.vector.tensor_scalar(coef[:, 0, :], th4[:, 0, :], 1.0, 1.0, ALU.mult, ALU.add))
                link(nc.vector.tensor_copy(coef[:, 1, :], th4[:, 1, :]))
                link(nc.vector.tensor_scalar(coef[:, 2:4, :], th4[:, 2:4, :], 0.5, None, ALU.mult))

        xin_in = [sem("xin_in0"), sem("xin_in1")]
        xin_free = sem("xin_free")
        stats_taken = sem("stats_taken")
        dve2 = sem("dve2")
        var2 = sem("var2")
        sd2 = sem("sd2")
        norm2 = sem("norm2")
        xn_ready = sem("xn_ready")
        xn_sent = [sem("xn_sent0"), sem("xn_sent1")]
        turned2 = sem("turned2")
        turned2_read = sem("turned2_read")
        logits_done = sem("logits_done")
        logits_read = sem("logits_read")
        counted = sem("counted")
        prefixed = sem("prefixed")
        slots_ready = sem("slots_ready")
        pads_ready = sem("pads_ready")
        pads_in = sem("pads_in")
        tab_ready = sem("tab_ready")
        tab_turned = sem("tab_turned")
        d_ready = sem("d_ready")
        zrows_set = sem("zrows_set")
        rstd2 = sem("rstd2")
        masked = sem("masked")
        e_ready = sem("e_ready")

        def pairs(eng, body):
            for u in range(2):
                body(u, 0, u, False)
            with eng.Fori(1, NGT // 2) as i:
                for u in range(2):
                    body(2 * i + u, i, u, False)
            body(NGT - 1, NGT // 2, 0, True)

        with nc.Block() as block:
            @block.sync
            def _(sp):
                for e in range(EARLY, MIDDLE):
                    load_expert(sp, e, weights_in)

                def load_x(g, i, u, last):
                    sp.wait_ge(xin_free, g + 1)
                    head = (GT - 1) * P
                    rows = LAST if last else P
                    sp.dma_start(x_in[:, u, 0:GT - 1, :],
                                 x[ds(g * (GT * P), head), :].rearrange("(t p) c -> p t c", p=P)
                                 ).then_inc(xin_in[u], 16)
                    sp.dma_start(x_in[0:rows, u, GT - 1, :], x[ds(g * (GT * P) + head, rows), :]
                                 ).then_inc(xin_in[u], 16)
                pairs(sp, load_x)
                sp.wait_ge(pads_ready, 1)
                sp.wait_ge(zrows_set, 1)
                with sp.Fori(0, E) as e:
                    row = sp.value_load(pad_i[0:1, ds(e, 1)], min_val=0, max_val=XROWS - P)
                    sp.dma_start(xs[ds(row, P), :], zrows).then_inc(pads_in, 16)
                sp.wait_ge(prefixed, NGT)
                for u in range(2):
                    sp.wait_ge(xn_sent[u], 16 * 2 * GT * (NGT - NGT // 2 if u == 0 else NGT // 2))
                for e in range(MIDDLE, E):
                    load_expert(sp, e, weights_in)
                sp.wait_ge(pads_in, 16 * E)

            @block.gpsimd
            def _(pool):
                def send(g, i, u, last):
                    pool.wait_ge(slots_ready, g + 1)
                    pool.sem_inc(pool_mark, 1)
                    for j in range(GT):
                        rows = LAST if last and j == GT - 1 else P
                        for k in range(2):
                            nc.gpsimd.indirect_dma_start(
                                out=xs[:, :], out_offset=bass.IndirectOffsetOnAxis(ap=slot_i[0:rows, u, j, k:k + 1], axis=0),
                                in_=xn[0:rows, u, j, :], in_offset=None).then_inc(xn_sent[u], 16)

                nc.gpsimd.memset(zrows, 0.0).then_inc(zrows_set, 1)
                pairs(pool, send)

            @block.scalar
            def _(act):
                def normalise(g, i, u, last):
                    act.wait_ge(var2, g + 1)
                    act.activation(sd[:, ds(g * GT, GT)], tmpa[:, ds(g * GT, GT)], ACT.Sqrt).then_inc(sd2, 1)
                    act.wait_ge(norm2, g + 1)
                    wait_past(act, xn_sent[u], (16 * 2 * GT) * i)
                    for j in range(GT):
                        row = XH[:, ds(g * GT + j, 1), :].rearrange("p o c -> p (o c)")
                        nc.scalar.activation(xn[:, u, j, :], row, ACT.Identity, bias=nmr[:, ds(g * GT + j, 1)],
                                             scale=rstd[:, ds(g * GT + j, 1)]).then_inc(xn_ready, 1)
                    wait_past(act, logits_done, g + 0)
                    for b in range(4):
                        n = 2 if b < 3 else 1
                        act.wait_ge(turned2, 4 * g + (b + 1))
                        act.activation(xnT[:, 2 * b:2 * b + n], PS[:, b, 0:n * C].rearrange("p (j k m) -> p j k m", j=n, k=2),
                                       ACT.Copy).then_inc(turned2_read, 1)
                pairs(act, normalise)
                act.wait_ge(d_ready, 1)
                act.activation(sd[:, :], tmpa[:, :], ACT.Exp).then_inc(e_ready, 1)

            @block.tensor
            def _(pe):
                def gate(g, i, u, last):
                    for b in range(4):
                        n = 2 if b < 3 else 1
                        pe.wait_ge(xn_ready, GT * g + (2 * b + n))
                        wait_past(pe, turned2_read, 4 * g + 0)
                        for j in range(n):
                            for k in range(2):
                                last_ins = nc.tensor.transpose(
                                    PS[:, b, j * C + k * P:j * C + (k + 1) * P],
                                    xn[:, u, 2 * b + j, :].rearrange("p (c k) -> p k c", k=2)[:, k, :], ident[:, :])
                        last_ins.then_inc(turned2, 1)
                    pe.wait_ge(turned2_read, 4 * g + 4)
                    wait_past(pe, logits_read, g + 0)
                    for j in range(GT):
                        for k in range(2):
                            last_ins = nc.tensor.matmul(PS[:, 4, j * E:(j + 1) * E], xnT[:, j, k, :], gw_sb[:, k, :],
                                                        start=(k == 0), stop=(k == 1))
                    last_ins.then_inc(logits_done, 1)
                    pe.wait_ge(counted, g + 1)
                    s = cnt_in[:, :, :].rearrange("p j e -> p (j e)")
                    nc.tensor.matmul(PS[:, 5, 0:(GT + 1) * E], upper[:, :], s, start=True, stop=False)
                    for j in range(GT):
                        o = PS[:, 5, (j + 1) * E:(GT + 1) * E].rearrange("p (j e) -> p j e", e=E)
                        last_ins = nc.tensor.matmul(o, onesb[:, :], cnt_in[:, j:j + 1, :].to_broadcast([P, GT - j, E]),
                                                    start=False, stop=(j == GT - 1))
                    last_ins.then_inc(prefixed, 1)
                pairs(pe, gate)
                pe.wait_ge(tab_ready, 1)
                nc.tensor.transpose(PS[0:1, 6, 0:P], et[:, 0:1], ident[:, :])
                nc.tensor.transpose(PS[0:1, 6, P:2 * P], et[:, 1:2], ident[:, :]).then_inc(tab_turned, 1)

            @block.vector
            def _(dve):
                link = linker(dve, dve2)
                dve.sem_inc(xin_free, 2)
                link(nc.vector.tensor_copy(carry[:, :], ecap[:, :]))
                A_STEPS, B_STEPS = 6 + 2, 3 + 1 + 2 + 2 + 4

                def affine(g, i, u):
                    rows = XH[:, ds(g * GT, GT), :]
                    cb = [coef[:, q, :].unsqueeze(1).to_broadcast([P, GT, C]) for q in range(4)]
                    link(nc.vector.tensor_tensor(branch, rows, cb[0], ALU.mult))
                    link(nc.vector.tensor_tensor(branch, branch, cb[2], ALU.add))
                    link(nc.vector.tensor_tensor(rows, rows, cb[1], ALU.mult))
                    link(nc.vector.tensor_tensor(rows, rows, cb[3], ALU.add))
                    link(nc.vector.tensor_tensor(rows, rows, branch, ALU.max))
                    dve.wait_ge(xin_in[u], 32 * i + 32)
                    link(nc.vector.tensor_tensor(rows, rows, x_in[:, u], ALU.add))
                    dve.sem_inc(xin_free, 1)
                    for j in range(GT):
                        ins = nc.vector.bn_stats(st2[:, j, :],
                                                 XH[:, ds(g * GT + j, 1), :].rearrange("p o c -> p (o c)"))
                    link(ins)
                    dve.sem_inc(stats_taken, 1)
                    for j in range(GT):
                        ins = nc.vector.bn_aggr(mv2[:, j, :], st2[:, j, :])
                    link(ins)
                    nc.vector.tensor_scalar(tmpa[:, ds(g * GT, GT)], mv2[:, :, 1],
                                            EPS, None, ALU.add).then_inc(var2, 1)

                def scale(g):
                    dve.wait_ge(sd2, g + 1)
                    nc.vector.reciprocal(rstd[:, ds(g * GT, GT)], sd[:, ds(g * GT, GT)]).then_inc(rstd2, 1)
                    dve.wait_ge(rstd2, g + 1)
                    nc.vector.scalar_tensor_tensor(nmr[:, ds(g * GT, GT)],
                                                   mv2[:, :, 0], -1.0,
                                                   rstd[:, ds(g * GT, GT)], ALU.mult, ALU.mult).then_inc(norm2, 1)

                def route(g, i, u, last=False):
                    dve.wait_ge(logits_done, g + 1)
                    link(nc.vector.tensor_tensor(logit[:, :, :], PS[:, 4, 0:GT * E].rearrange("p (j e) -> p j e", e=E),
                                                 gateb_bc[:, :].unsqueeze(1).to_broadcast([P, GT, E]), ALU.add))
                    dve.sem_inc(logits_read, 1)
                    for j in range(GT):
                        ins = nc.vector.max(top[:, j, :], logit[:, j, :])
                    link(ins)
                    nc.vector.tensor_scalar(TOPV[:, ds(g * GT, GT), :], top[:, :, 0:2], 1.0, None, ALU.mult)
                    for j in range(GT):
                        ins = nc.vector.max_index(topi[:, j, :], top[:, j, :], logit[:, j, :])
                    link(ins)
                    link(nc.vector.tensor_scalar(IDX[:, ds(g * GT, GT), :], topi[:, :, 0:2], 1.0, None, ALU.mult))
                    for k in range(2):
                        link(nc.vector.tensor_tensor(
                            oh[:, k], iota16[:, :].unsqueeze(1).to_broadcast([P, GT, E]),
                            IDX[:, ds(g * GT, GT), k:k + 1].to_broadcast([P, GT, E]), ALU.is_equal))
                    if last:
                        for k in range(2):
                            nc.vector.tensor_scalar(oh[:, k, GT - 1, :], oh[:, k, GT - 1, :], rowmask[:, :], None,
                                                    ALU.mult).then_inc(masked, 1)
                        dve.wait_ge(masked, 2)
                    nc.vector.tensor_tensor(cnt_in[:, 0:GT, :], oh[:, 0], oh[:, 1], ALU.add).then_inc(counted, 1)
                    dve.wait_ge(prefixed, g + 1)
                    link(nc.vector.tensor_tensor(posq[:, :, :], PS[:, 5, 0:GT * E].rearrange("p (j e) -> p j e", e=E),
                                                 carry[:, :].unsqueeze(1).to_broadcast([P, GT, E]), ALU.add))
                    link(nc.vector.tensor_tensor(carry[:, :], PS[:, 5, GT * E:(GT + 1) * E], carry[:, :], ALU.add))
                    for k in range(2):
                        link(nc.vector.tensor_tensor(prodq[:, :, :], oh[:, k], posq[:, :, :], ALU.mult))
                        link(nc.vector.tensor_reduce(SLOT[:, ds(g * GT, GT), k:k + 1].rearrange("p t o -> p (t o)"),
                                                     prodq[:, :, :], AX.X, ALU.add))
                    wait_past(dve, xn_sent[u], (16 * 2 * GT) * i)
                    nc.vector.tensor_scalar(slot_i[:, u], SLOT[:, ds(g * GT, GT), :], 1.0, None, ALU.mult).then_inc(slots_ready, 1)

                affine(0, 0, 0)
                scale(0)
                start = link.state[1]
                def pair(i):
                    link.rebase(i * (2 * (A_STEPS + B_STEPS)) + start)
                    affine(2 * i + 1, i, 1)
                    route(2 * i, i, 0)
                    scale(2 * i + 1)
                    affine(2 * i + 2, i + 1, 0)
                    route(2 * i + 1, i, 1)
                    scale(2 * i + 2)
                    assert link.state[1] == 2 * (A_STEPS + B_STEPS), link.state
                pair(0)
                with dve.Fori(1, NGT // 2) as i:
                    pair(i)
                link.rebase(start + (NGT // 2) * 2 * (A_STEPS + B_STEPS))
                route(NGT - 1, NGT // 2, 0, True)
                nc.vector.tensor_copy(pad_i[:, :], carry[0:1, :]).then_inc(pads_ready, 1)
                link(nc.vector.tensor_tensor(p16[:, :], carry[:, :], ecap[:, :], ALU.subtract))
                link(nc.vector.tensor_scalar(p16[:, :], p16[:, :], float(P - 1), None, ALU.add))
                link(nc.vector.tensor_copy(cnti[:, :], p16[:, :]))
                link(nc.vector.tensor_scalar(cnti[:, :], cnti[:, :], LO_BITS, None, ALU.logical_shift_right))
                link(nc.vector.tensor_copy(nt16[:, :], cnti[:, :]))
                link(nc.vector.tensor_copy(cum[:, 0, :], nt16[:, :]))
                cur = 0
                for s in (1, 2, 4, 8):
                    link(nc.vector.tensor_copy(cum[:, 1 - cur, 0:s], cum[:, cur, 0:s]))
                    link(nc.vector.tensor_tensor(cum[:, 1 - cur, s:E], cum[:, cur, s:E], cum[:, cur, 0:E - s], ALU.add))
                    cur = 1 - cur
                link(nc.vector.tensor_scalar(fin16[:, :], cum[:, cur, :], iota_p[:, :], None, ALU.is_le))
                link(nc.vector.tensor_reduce(et[:, 0:1], fin16[:, :], AX.X, ALU.add))
                link(nc.vector.tensor_tensor(p16[:, :], fin16[:, :], nt16[:, :], ALU.mult))
                link(nc.vector.tensor_reduce(et[:, 2:3], p16[:, :], AX.X, ALU.add))
                link(nc.vector.tensor_tensor(et[:, 2:3], iota_p[:, :], et[:, 2:3], ALU.subtract))
                link(nc.vector.tensor_scalar(et[:, 3:4], et[:, 0:1], float(CAP), None, ALU.mult))
                link(nc.vector.scalar_tensor_tensor(et[:, 1:2], et[:, 2:3], float(P), et[:, 3:4], ALU.mult, ALU.add))
                link(nc.vector.tensor_scalar(et[:, 3:4], et[:, 0:1], float(E) - 0.5, None, ALU.is_lt))
                link(nc.vector.tensor_tensor(et[:, 1:2], et[:, 1:2], et[:, 3:4], ALU.mult))
                nc.vector.tensor_scalar(et[:, 0:1], et[:, 0:1], float(E - 1), None, ALU.min).then_inc(tab_ready, 1)
                dve.wait_ge(tab_turned, 1)
                link(nc.vector.tensor_copy(tile_e[:, :], PS[0:1, 6, 0:P]))
                link(nc.vector.tensor_copy(tile_r[:, :], PS[0:1, 6, P:2 * P]))
                link(nc.vector.tensor_tensor(dbase[:, :], cum[:, cur, :], nt16[:, :], ALU.subtract))
                link(nc.vector.tensor_scalar(dbase[:, :], dbase[:, :], float(P), None, ALU.mult))
                link(nc.vector.tensor_tensor(dbase[:, :], dbase[:, :], ecap[:, :], ALU.subtract))
                nc.vector.tensor_tensor(tmpa[:, :], TOPV[:, :, 1:2].rearrange("p t o -> p (t o)"),
                                        TOPV[:, :, 0:1].rearrange("p t o -> p (t o)"), ALU.subtract).then_inc(d_ready, 1)
                dve.wait_ge(e_ready, 1)
                link(nc.vector.tensor_scalar(tmpb[:, :], sd[:, :], 1.0, None, ALU.add))
                link(nc.vector.reciprocal(WT[:, 0, :], tmpb[:, :]))
                link(nc.vector.tensor_tensor(WT[:, 1, :], WT[:, 0, :], sd[:, :], ALU.mult))

        x3_in = [sem("x3_in0"), sem("x3_in1")]
        x_turned = sem("x_turned")
        xt_copied = sem("xt_copied")
        mm1_done = sem("mm1_done")
        h_copied = sem("h_copied")
        h_turned = sem("h_turned")
        relu_act = sem("relu_act")
        relu_dve = sem("relu_dve")
        mm2_done = sem("mm2_done")
        o_copied = sem("o_copied")
        o_sent = [sem("o_sent0"), sem("o_sent1")]
        pool3 = sem("pool3")

        with nc.Block() as block:
            def odd_even(eng, body):
                body(1, 1, 0)
                body(2, 0, 1)
                with eng.Fori(1, (MT - 2) // 2) as i:
                    body(2 * i + 1, 1, i)
                    body(2 * i + 2, 0, i + 1)

            @block.sync
            def _(sp):
                def load(t, u):
                    row = sp.value_load(tile_r[0:1, ds(t, 1)], min_val=0, max_val=XROWS - P)
                    sp.dma_start(X3[:, u, :], xs[ds(row, P), :]).then_inc(x3_in[u], 16)

                def store(t, u):
                    sp.wait_ge(o_copied, t + 3)
                    sp.dma_start(ys[ds(t * P, P), :], O3[:, u, :]).then_inc(o_sent[u], 16)

                load(0, 0)
                load(1, 1)
                sp.wait_ge(x_turned, 1)
                load(2, 0)
                sp.wait_ge(x_turned, 2)
                load(3, 1)
                store(0, 0)
                with sp.Fori(1, MT // 2 - 1) as i:
                    for u in range(2):
                        sp.wait_ge(x_turned, 2 * i + (u + 1))
                        load(2 * i + (u + 2), u)
                        store(2 * i + (u - 1), 1 - u)
                store(MT - 3, 1)
                store(MT - 2, 0)
                store(MT - 1, 1)
                for u in range(2):
                    sp.wait_ge(o_sent[u], 16 * (MT // 2))

            @block.tensor
            def _(pe):
                def turn_x(t, u, half):
                    pe.wait_ge(x3_in[u], 16 * half + 16)
                    cols = X3[:, u, :].rearrange("p (c k) -> p k c", k=2)
                    for k in range(2):
                        last = nc.tensor.transpose(PS[:, u, k * P:(k + 1) * P], cols[:, k, :], ident[:, :])
                    last.then_inc(x_turned, 1)

                def up(t, u, e_col):
                    pe.wait_ge(xt_copied, t + 1)
                    for k in range(2):
                        last = nc.tensor.matmul(PS[:, 2 + u, :], XT3[:, u, k, :], wt1(e_col, k),
                                                start=(k == 0), stop=(k == 1))
                    last.then_inc(mm1_done, 1)

                def turn_h(t, u):
                    pe.wait_ge(h_copied, t + 1)
                    cols = H3[:, u, :].rearrange("p (c j) -> p j c", j=4)
                    for j in range(4):
                        last = nc.tensor.transpose(PS[:, 4 + j // 2, (j % 2) * P:(j % 2 + 1) * P], cols[:, j, :], ident[:, :])
                    last.then_inc(h_turned, 1)

                def down(t, u, e_col):
                    pe.wait_ge(relu_act, t + 1)
                    pe.wait_ge(relu_dve, t + 1)
                    pe.wait_ge(o_copied, t + 1)
                    for j in range(4):
                        last = nc.tensor.matmul(PS[:, 6 + u, 0:C], HT3[:, u, j, :], wt2(e_col, j),
                                                start=(j == 0), stop=(j == 3))
                    last.then_inc(mm2_done, 1)

                def expert_cols(t):
                    return pe.value_load(tile_e[0:1, ds(t, 1)], min_val=0, max_val=E - 1) * WCOLS

                pe.sem_inc(o_copied, 2)
                pe.wait_ge(weights_in, 32 * E)
                turn_x(0, 0, 0)
                turn_x(1, 1, 0)
                up(0, 0, expert_cols(0))
                turn_h(0, 0)

                def step(t, u, i, cols, cols_before):
                    wait_past(pe, h_copied, t - 1)
                    up(t, u, cols)
                    pe.wait_ge(xt_copied, t + 0)
                    turn_x(t + 1, 1 - u, i + 1 if u == 1 else i)
                    down(t - 1, 1 - u, cols_before)
                    turn_h(t, u)

                def pair(i):
                    c = [expert_cols(2 * i + n) for n in range(3)]
                    step(2 * i + 1, 1, i, c[1], c[0])
                    step(2 * i + 2, 0, i + 1, c[2], c[1])
                pair(0)
                with pe.Fori(1, (MT - 2) // 2) as i:
                    pair(i)
                pe.wait_ge(h_copied, MT - 2)
                up(MT - 1, 1, expert_cols(MT - 1))
                down(MT - 2, 0, expert_cols(MT - 2))
                turn_h(MT - 1, 1)
                down(MT - 1, 1, expert_cols(MT - 1))

            @block.scalar
            def _(act):
                def copy_x(t, u):
                    act.wait_ge(x_turned, t + 1)
                    act.activation(XT3[:, u], PS[:, u, 0:C].rearrange("p (k m) -> p k m", k=2), ACT.Copy
                                   ).then_inc(xt_copied, 1)

                def relu(t, u):
                    act.wait_ge(h_turned, t + 1)
                    e = act.value_load(tile_e[0:1, ds(t, 1)], min_val=0, max_val=E - 1)
                    for j in (0, 1):
                        last = act.activation(HT3[:, u, j, :], PS[:, 4 + j // 2, (j % 2) * P:(j % 2 + 1) * P], ACT.Relu,
                                              bias=b1T[:, ds(e, 1), j])
                    last.then_inc(relu_act, 1)

                copy_x(0, 0)
                copy_x(1, 1)
                relu(0, 0)

                def step(t, u, i):
                    act.wait_ge(mm1_done, t + 0)
                    copy_x(t + 1, 1 - u)
                    wait_past(act, mm2_done, t - 1)
                    relu(t, u)
                odd_even(act, step)
                act.wait_ge(mm2_done, MT - 2)
                relu(MT - 1, 1)

            @block.vector
            def _(dve):
                def copy_h(t, u):
                    dve.wait_ge(mm1_done, t + 1)
                    nc.vector.tensor_copy(H3[:, u, :], PS[:, 2 + u, :]).then_inc(h_copied, 1)

                def relu(t, u):
                    dve.wait_ge(h_turned, t + 1)
                    e = dve.value_load(tile_e[0:1, ds(t, 1)], min_val=0, max_val=E - 1)
                    for j in (2, 3):
                        last = nc.vector.tensor_scalar(HT3[:, u, j, :], PS[:, 4 + j // 2, (j % 2) * P:(j % 2 + 1) * P],
                                                       b1T[:, ds(e, 1), j], 0.0, ALU.add, ALU.max)
                    last.then_inc(relu_dve, 1)

                def copy_o(t, u, half):
                    dve.wait_ge(mm2_done, t + 1)
                    wait_past(dve, o_sent[u], 16 * half)
                    nc.vector.tensor_copy(O3[:, u, :], PS[:, 6 + u, 0:C]).then_inc(o_copied, 1)

                copy_h(0, 0)
                relu(0, 0)

                def step(t, u, i):
                    wait_past(dve, h_turned, t - 1)
                    copy_h(t, u)
                    copy_o(t - 1, 1 - u, i if u == 1 else i - 1)
                    relu(t, u)
                odd_even(dve, step)
                dve.wait_ge(h_turned, MT - 2)
                copy_h(MT - 1, 1)
                copy_o(MT - 2, 0, MT // 2 - 1)
                relu(MT - 1, 1)
                copy_o(MT - 1, 1, MT // 2 - 1)

            @block.gpsimd
            def _(pool):
                link = linker(pool, pool3)
                PER = 2 * 9 + 2
                with pool.Fori(0, NGT) as g:
                    link.rebase(g * PER)
                    tiles = ds(g * GT, GT)
                    for k in range(2):
                        link(nc.gpsimd.tensor_tensor(oh[:, k], iota16[:, :].unsqueeze(1).to_broadcast([P, GT, E]),
                                                     IDX[:, tiles, k:k + 1].to_broadcast([P, GT, E]), ALU.subtract))
                        pool.sem_inc(pool_mark, 1)
                        link(nc.gpsimd.tensor_scalar(oh[:, k], oh[:, k], 0.0, None, ALU.is_equal))
                        link(nc.gpsimd.tensor_tensor(prodq[:, :, :], oh[:, k],
                                                     dbase[:, :].unsqueeze(1).to_broadcast([P, GT, E]), ALU.mult))
                        for half in (8, 4, 2, 1):
                            link(nc.gpsimd.tensor_tensor(prodq[:, :, 0:half], prodq[:, :, 0:half],
                                                         prodq[:, :, half:2 * half], ALU.add))
                        link(nc.gpsimd.tensor_tensor(SLOT[:, tiles, k:k + 1], SLOT[:, tiles, k:k + 1],
                                                     prodq[:, :, 0:1], ALU.add))
                        link(nc.gpsimd.tensor_tensor(oh[:, k], oh[:, k],
                                                     WT[:, k, tiles].unsqueeze(2).to_broadcast([P, GT, E]), ALU.mult))
                    link(nc.gpsimd.tensor_tensor(GM[:, tiles, :], oh[:, 0], oh[:, 1], ALU.add))
                    link(nc.gpsimd.tensor_copy(SLOTI[:, tiles, :], SLOT[:, tiles, :]))
                    assert link.state[1] == PER, link.state

        affine_in = sem("affine_in")
        idx_copied = sem("idx_copied")
        picks_in = [sem("picks_in0"), sem("picks_in1")]
        x1b_ready = sem("x1b_ready")
        gm_copied = sem("gm_copied")
        gm_turned = sem("gm_turned")
        gmT_copied = sem("gmT_copied")
        xn4_ready = sem("xn4_ready")
        base_done = sem("base_done")
        acc_step = sem("acc_step")
        acc_free = sem("acc_free")
        var4 = sem("var4")
        sd4_ready = sem("sd4_ready")
        norm4 = sem("norm4")
        y4_ready = sem("y4_ready")
        out_ready = sem("out_ready")
        out_sent = [sem("out_sent0"), sem("out_sent1")]
        base_free = sem("base_free")
        rs4_ready = sem("rs4_ready")
        y4_free = sem("y4_free")
        out_ready_free = sem("out_ready_free")

        with nc.Block() as block:
            @block.sync
            def _(sp):
                sp.dma_start(gamma_bc, gamma.partition_broadcast(P)).then_inc(affine_in, 16)
                sp.dma_start(beta_bc, beta.partition_broadcast(P)).then_inc(affine_in, 16)

                def store(t, u, rows=P):
                    sp.wait_ge(out_ready, t + 1)
                    sp.dma_start(out[ds(t * P, rows), :], out4[0:rows, u, :]).then_inc(out_sent[u], 16)
                with sp.Fori(0, NT // 2) as i:
                    store(2 * i, 0)
                    store(2 * i + 1, 1)
                store(NT - 1, 0, LAST)
                sp.wait_ge(out_sent[0], 16 * (NT // 2 + 1))
                sp.wait_ge(out_sent[1], 16 * (NT // 2))

            @block.gpsimd
            def _(pool):
                nc.gpsimd.memset(pick0[96:P, 0, :], 0.0).then_inc(idx_copied, 1)
                nc.gpsimd.memset(pick1[96:P, 0, :], 0.0).then_inc(idx_copied, 1)
                pool.wait_ge(idx_copied, 2)
                pool.wait_ge(affine_in, 32)
                pool.sem_inc(acc_free, 2)
                pool.sem_inc(out_ready_free, 2)

                def pick(t, u, rows=P):
                    pool.wait_ge(acc_free, t + 1)
                    nc.gpsimd.tensor_copy(gidx[:, 2 * u:2 * u + 2],
                                          SLOTI[:, ds(t, 1), :].rearrange("p o k -> p (o k)")).then_inc(idx_copied, 1)
                    pool.wait_ge(idx_copied, t + 3)
                    pool.sem_inc(pool_mark, 1)
                    for k, into in ((0, pick0), (1, pick1)):
                        nc.gpsimd.indirect_dma_start(
                            out=into[0:rows, u, :], out_offset=None, in_=ys[:, :],
                            in_offset=bass.IndirectOffsetOnAxis(ap=gidx[0:rows, 2 * u + k:2 * u + k + 1], axis=0)
                        ).then_inc(picks_in[u], 16)
                    pool.wait_ge(out_ready_free, t + 1)
                    nc.gpsimd.tensor_tensor(x1b4[:, u, :], XH[:, ds(t, 1), :].rearrange("p o c -> p (o c)"),
                                            beta_bc, ALU.add).then_inc(x1b_ready, 1)
                with pool.Fori(0, NT // 2) as i:
                    pick(2 * i, 0)
                    pick(2 * i + 1, 1)
                pick(NT - 1, 0, LAST)

            @block.scalar
            def _(act):
                def front(t, u):
                    act.wait_ge(base_free, t + 1)
                    act.activation(gm_s[:, u, :], GM[:, ds(t, 1), :].rearrange("p o e -> p (o e)"), ACT.Copy
                                   ).then_inc(gm_copied, 1)
                    act.activation(xn4[:, u, :], XH[:, ds(t, 1), :].rearrange("p o c -> p (o c)"), ACT.Identity,
                                   bias=nmr[:, ds(t, 1)], scale=rstd[:, ds(t, 1)]).then_inc(xn4_ready, 1)
                    act.wait_ge(gm_turned, t + 1)
                    act.activation(gmT[0:E, u, :], PS[0:E, u, 0:P], ACT.Copy).then_inc(gmT_copied, 1)

                def back(t, u):
                    act.wait_ge(var4, t + 1)
                    act.activation(sd4[:, u, :], ve4[:, u, :], ACT.Sqrt).then_inc(sd4_ready, 1)
                    act.wait_ge(norm4, t + 1)
                    act.wait_ge(y4_free, t + 1)
                    act.activation(y4[:, u, :], acc4[:, u, :], ACT.Identity, bias=nm4[:, u, :],
                                   scale=rs4[:, u, :]).then_inc(y4_ready, 1)
                front(0, 0)
                with act.Fori(0, NT // 2) as i:
                    front(2 * i + 1, 1)
                    back(2 * i, 0)
                    front(2 * i + 2, 0)
                    back(2 * i + 1, 1)
                back(NT - 1, 0)

            @block.tensor
            def _(pe):
                pe.sem_inc(base_free, 2)

                def base(t, u):
                    pe.wait_ge(gm_copied, t + 1)
                    nc.tensor.transpose(PS[0:E, u, 0:P], gm_s[:, u, :], ident[:, :]).then_inc(gm_turned, 1)
                    pe.wait_ge(gmT_copied, t + 1)
                    nc.tensor.matmul(PS[:, 2 + u, 0:C], gmT[0:E, u, :], b2_sb[:, :], start=True, stop=False)
                    pe.wait_ge(xn4_ready, t + 1)
                    nc.tensor.matmul(PS[:, 2 + u, 0:C], ident[:, :], xn4[:, u, :], start=False, stop=True
                                     ).then_inc(base_done, 1)
                with pe.Fori(0, NT // 2) as i:
                    base(2 * i, 0)
                    base(2 * i + 1, 1)
                base(NT - 1, 0)

            @block.vector
            def _(dve):
                dve.wait_ge(affine_in, 32)
                dve.sem_inc(y4_free, 2)

                def gather_sum(t, u, half):
                    dve.wait_ge(base_done, t + 1)
                    dve.wait_ge(picks_in[u], 32 * half + 32)
                    nc.vector.scalar_tensor_tensor(acc4[:, u, :], pick0[:, u, :], WT[:, 0, ds(t, 1)],
                                                   PS[:, 2 + u, 0:C], ALU.mult, ALU.add).then_inc(base_free, 1)
                    dve.wait_ge(base_free, t + 3)
                    nc.vector.scalar_tensor_tensor(acc4[:, u, :], pick1[:, u, :], WT[:, 1, ds(t, 1)],
                                                   acc4[:, u, :], ALU.mult, ALU.add).then_inc(acc_step, 1)
                    dve.wait_ge(acc_step, 3 * t + 1)
                    nc.vector.bn_stats(st4[:, u, :], acc4[:, u, :]).then_inc(acc_step, 1)
                    dve.wait_ge(acc_step, 3 * t + 2)
                    dve.sem_inc(acc_free, 1)
                    nc.vector.bn_aggr(mv4[:, u, :], st4[:, u, :]).then_inc(acc_step, 1)
                    dve.wait_ge(acc_step, 3 * t + 3)
                    nc.vector.tensor_scalar(ve4[:, u, :], mv4[:, u, 1:2], EPS, None, ALU.add).then_inc(var4, 1)

                def scales(t, u):
                    dve.wait_ge(sd4_ready, t + 1)
                    nc.vector.reciprocal(rs4[:, u, :], sd4[:, u, :]).then_inc(rs4_ready, 1)
                    dve.wait_ge(rs4_ready, t + 1)
                    nc.vector.scalar_tensor_tensor(nm4[:, u, :], mv4[:, u, 0:1], -1.0, rs4[:, u, :],
                                                   ALU.mult, ALU.mult).then_inc(norm4, 1)

                def finish(t, u, half):
                    dve.wait_ge(y4_ready, t + 1)
                    wait_past(dve, out_sent[u], 16 * half)
                    nc.vector.tensor_tensor(out4[:, u, :], y4[:, u, :], gamma_bc, ALU.mult).then_inc(y4_free, 1)
                    dve.wait_ge(y4_free, t + 3)
                    dve.wait_ge(x1b_ready, t + 1)
                    nc.vector.tensor_tensor(out4[:, u, :], out4[:, u, :], x1b4[:, u, :], ALU.add
                                            ).then_inc(out_ready, 1)
                    dve.wait_ge(out_ready, t + 1)
                    dve.sem_inc(out_ready_free, 1)

                gather_sum(0, 0, 0)
                scales(0, 0)
                def pair(i):
                    gather_sum(2 * i + 1, 1, i)
                    finish(2 * i, 0, i)
                    scales(2 * i + 1, 1)
                    gather_sum(2 * i + 2, 0, i + 1)
                    finish(2 * i + 1, 1, i)
                    scales(2 * i + 2, 0)
                pair(0)
                with dve.Fori(1, NT // 2) as i:
                    pair(i)
                finish(NT - 1, 0, NT // 2)


_INS = ['x', 'src', 'dst', 'L0_gnn_W1', 'L0_gnn_b1', 'L0_gnn_W2', 'L0_gnn_b2', 'L0_ffn_gate_w', 'L0_ffn_gate_b',
        'L0_ffn_w1', 'L0_ffn_b1', 'L0_ffn_w2', 'L0_ffn_b2', 'L0_ffn_gamma', 'L0_ffn_beta']


def kernel(**inputs):
    import numpy as _np
    import concourse.bacc as _bacc
    from concourse import mybir as _mybir
    from concourse.bass_utils import run_bass_kernel_spmd as _run

    nc = _bacc.Bacc("TRN2", target_bir_lowering=False, num_devices=1)
    arrays, args = {}, []
    for name in _INS:
        a = _np.ascontiguousarray(inputs[name])
        arrays[f"in_{name}"] = a
        args.append(nc.dram_tensor(f"in_{name}", a.shape, _mybir.dt.from_np(a.dtype), kind="ExternalInput").ap())
    args.append(nc.dram_tensor("out_0", (N, C), _mybir.dt.float32, kind="ExternalOutput").ap())
    build(nc, *args)
    r = _run(nc, [arrays], core_ids=[0])
    return r.results[0]["out_0"]
```

```python
import concourse.bass as bass
from concourse import mybir
from contextlib import ExitStack

P = 128
N, C = 6250, 256
EDGES = 106250
HID = 64
E, F = 16, 512
NT = -(-N // P)
LAST = N - (NT - 1) * P
EPS = 1e-5

EC = EDGES // P
ETAIL = EDGES - EC * P
GC = 32
NCH = 832
NG = NCH // GC
PAD_INDEX = 8191
LO_BITS = 7
BLK = -(-NCH // P)

GT = 7
NGT = NT // GT

CAP = 6400
MT = 114
XROWS = E * CAP
WCOLS = 2 * C * F // P
assert MT * P >= 2 * N + E * (P - 1) and MT % 2 == 0 and N + P <= CAP
assert NG * GC == NCH and NG % 2 == 0 and NGT * GT == NT and NGT % 2 == 1


def build(nc, x, src, dst, gW1, gb1, gW2, gb2, gate_w, gate_b, w1, b1, w2, b2, gamma, beta, out):
    fp32, bf16, fp16 = mybir.dt.float32, mybir.dt.bfloat16, mybir.dt.float16
    i32, u32 = mybir.dt.int32, mybir.dt.uint32
    ALU = mybir.AluOpType
    ACT = mybir.ActivationFunctionType
    AX = mybir.AxisListType
    ds = bass.ds

    ctx = ExitStack()
    with ctx:
        def sb(name, shape, dt):
            return ctx.enter_context(nc.sbuf_tensor(name, shape, dt))

        def sem(name):
            return ctx.enter_context(nc.semaphore(name))

        lo_rows = nc.dram_tensor("lo_rows", (NCH, P), bf16, kind="Internal").ap()
        xs = nc.dram_tensor("xs", (XROWS, C), fp32, kind="Internal").ap()
        ys = nc.dram_tensor("ys", (MT * P, C), fp32, kind="Internal").ap()

        W = sb("W", [P, E * WCOLS], fp32)
        XH = sb("XH", [P, NT, C], fp32)
        RB = 14336
        R = sb("R", [P, RB // 4], fp32)

        def carve(base, start):
            at = [start]

            def take(dims, dt):
                size = {fp32: 4, i32: 4, u32: 4, bf16: 2, fp16: 2}[dt]
                n = size
                for d in dims:
                    n *= d
                n = -(-n // 4) * 4
                v = base[:, at[0] // 4:(at[0] + n) // 4]
                if dt != fp32:
                    v = v.bitcast(dt)
                at[0] += n
                if len(dims) == 2:
                    v = v.rearrange("p (a b) -> p a b", a=dims[0])
                elif len(dims) == 3:
                    v = v.rearrange("p (a b c) -> p a b c", a=dims[0], b=dims[1])
                elif len(dims) == 4:
                    v = v.rearrange("p (a b c d) -> p a b c d", a=dims[0], b=dims[1], c=dims[2])
                return v
            return take, at

        EARLY = 4
        MIDDLE = 9
        take, at = carve(W, EARLY * WCOLS * 4)
        iota_lo = take([P, GC], bf16)
        iota_hi = take([NT, GC], bf16)
        oh_lo = take([2, P, GC], bf16)
        oh_hi = take([2, NT, GC], bf16)
        oh_src = take([2, NT, GC], bf16)
        ints = at[0]
        oh_t = take([2, GC * P], bf16)
        lo_bc = take([2, GC * P], bf16)
        picked = take([GC, NT], fp32)
        weighted = take([2, 2, NT, GC], fp16)
        assert at[0] <= E * WCOLS * 4
        take, at = carve(W, ints)
        dst_i = take([NCH], i32)
        src_i = take([NCH], i32)
        hi_i = take([NCH], i32)
        lo_i = take([NCH], i32)
        take, at = carve(R, 0)
        dlo = take([NCH], bf16)
        dhi = take([NCH], bf16)
        slo = take([NCH], bf16)
        shi = take([NCH], bf16)
        loT = take([BLK, P], bf16)
        junk = take([C], fp32)
        g_val = take([GC], fp32)
        g_rest = take([GC], fp32)
        g_two = take([2, GC], fp16)
        gW1_sb = take([2, HID], fp32)
        th_bc = take([P], fp32)
        lnsum = take([NT], fp32)
        lnsq = take([NT], fp32)
        nmean = take([NT], fp32)
        deg = take([NT], fp32)
        assert at[0] <= RB
        take, at = carve(W, EARLY * WCOLS * 4)
        gb2_bc = take([4 * C], fp32)
        theta = take([4 * C], fp32)
        gW2_sb = take([4 * C], fp32)
        take, at = carve(W, MIDDLE * WCOLS * 4)
        x_in = take([2, GT, C], fp32)
        branch = take([GT, C], fp32)
        xn = take([2, GT, C], fp32)
        xnT = take([GT, 2, P], fp32)
        assert at[0] <= E * WCOLS * 4
        take, at = carve(R, 0)
        zrows = take([C], fp32)
        coef = take([4, C], fp32)
        assert at[0] <= RB
        take, at = carve(R, 0)
        X3 = take([2, C], fp32)
        XT3 = take([2, 2, P], fp32)
        H3 = take([2, F], fp32)
        HT3 = take([2, 4, P], fp32)
        O3 = take([2, C], fp32)
        assert at[0] <= RB
        take, at = carve(W, 0)
        picks = [take([GT, 2, C], fp32) for _ in range(2)]
        xn4 = take([2, GT, C], fp32)
        acc4 = take([2, GT, C], fp32)
        y4 = take([2, GT, C], fp32)
        out4 = take([2, GT, C], fp32)
        gm_s = take([2, GT, E], fp32)
        gmT = take([2, GT, P], fp32)
        gamma_bc = take([C], fp32)
        beta_bc = take([C], fp32)
        st4 = take([GT, 6], fp32)
        mv4 = take([2, GT, 2], fp32)
        ve4 = take([2, GT], fp32)
        sd4 = take([2, GT], fp32)
        rs4 = take([2, GT], fp32)
        nm4 = take([2, GT], fp32)
        gidx = [take([GT * 2], i32) for _ in range(2)]
        assert at[0] <= E * WCOLS * 4

        ident = sb("ident", [P, P], fp32)
        identb = sb("identb", [P, P], bf16)
        upper = sb("upper", [P, P], bf16)
        onesb = sb("onesb", [P, P], bf16)
        zerob = sb("zerob", [P, P], bf16)
        iota_p = sb("iota_p", [P, 1], fp32)
        iota16 = sb("iota16", [P, E], fp32)
        rowmask = sb("rowmask", [P, 1], fp32)
        gw_sb = sb("gw_sb", [P, 2, E], fp32)
        gateb_bc = sb("gateb_bc", [P, E], fp32)
        gb1_col = sb("gb1_col", [HID, 1], fp32)
        b1T = sb("b1T", [P, E, 4], fp32)
        b2_sb = sb("b2_sb", [E, C], fp32)
        nmr = sb("nmr", [P, NT], fp32)
        rstd = sb("rstd", [P, NT], fp32)
        sd = sb("sd", [P, NT], fp32)
        dis = sb("dis", [P, NT], fp32)
        tmpa = sb("tmpa", [P, NT], fp32)
        tmpb = sb("tmpb", [P, NT], fp32)
        dis3 = sb("dis3", [P, 3, NT], bf16)
        wts = sb("wts", [P, NT], fp32)
        vcol = sb("vcol", [P, 2], fp32)
        th = sb("th", [HID, 1], fp32)
        mv2 = sb("mv2", [P, GT, 2], fp32)
        st2 = sb("st2", [P, GT, 6], fp32)
        logit = sb("logit", [P, GT, E], fp32)
        top = sb("top", [P, GT, 8], fp32)
        topi = sb("topi", [P, GT, 8], u32)
        IDX = sb("IDX", [P, NT, 2], fp32)
        TOPV = sb("TOPV", [P, NT, 2], fp32)
        SLOT = sb("SLOT", [P, NT, 2], fp32)
        WT = sb("WT", [P, 2, NT], fp32)
        oh = sb("oh", [P, 2, GT, E], fp32)
        cnt_in = sb("cnt_in", [P, GT + 1, E], bf16)
        posq = sb("posq", [P, GT, E], fp32)
        prodq = sb("prodq", [P, GT, E], fp32)
        carry = sb("carry", [P, E], fp32)
        ecap = sb("ecap", [P, E], fp32)
        slot_i = sb("slot_i", [P, 2, GT, 2], i32)
        pad_i = sb("pad_i", [1, E], i32)
        cnti = sb("cnti", [P, E], i32)
        nt16 = sb("nt16", [P, E], fp32)
        cum = sb("cum", [P, 2, E], fp32)
        fin16 = sb("fin16", [P, E], fp32)
        p16 = sb("p16", [P, E], fp32)
        et = sb("et", [P, 4], fp32)
        tile_e = sb("tile_e", [1, P], i32)
        tile_r = sb("tile_r", [1, P], i32)
        dbase = sb("dbase", [P, E], fp32)
        GM = sb("GM", [P, NT, E], fp32)
        SLOTI = sb("SLOTI", [P, NT, 2], i32)

        PS = ctx.enter_context(nc.psum_tensor("PS", [P, 8, 512], fp32))

        def wt1(e_col, k):
            return W[:, ds(e_col + k * F, F)]

        def wt2(e_col, j):
            return W[:, ds(e_col + 2 * F + j * C, C)]

        def load_expert(eng, e, done):
            eng.dma_start(W[:, e * WCOLS:e * WCOLS + 2 * F],
                          w1[e].rearrange("(p k) f -> p (k f)", k=2)).then_inc(done, 16)
            eng.dma_start(W[:, e * WCOLS + 2 * F:(e + 1) * WCOLS],
                          w2[e].rearrange("(p j) h -> p (j h)", j=4)).then_inc(done, 16)

        weights_in = sem("weights_in")
        late_in = sem("late_in")
        experts_ready = sem("experts_ready")
        wait_mark = sem("wait_mark")

        def linker(eng, signal, start=0):
            state = [start, 0]

            def link(ins):
                state[1] += 1
                ins.then_inc(signal, 1)
                eng.wait_ge(signal, state[0] + state[1])

            def rebase(base):
                state[0], state[1] = base, 0
            link.rebase = rebase
            link.state = state
            return link

        def wait_past(eng, signal, count):
            if not isinstance(count, int) or count > 0:
                eng.wait_ge(signal, count)

        consts_set = sem("consts_set")
        pads_set = sem("pads_set")
        idx_in = sem("idx_in")
        x_loaded = sem("x_loaded")
        small_in = sem("small_in")
        gb2_in = sem("gb2_in")
        dve_step = sem("dve_step")
        act_step = sem("act_step")
        idx_split = sem("idx_split")
        lo_turned = sem("lo_turned")
        loT_copied = sem("loT_copied")
        lo_stored = sem("lo_stored")
        lo_bc_in = [sem("lo_bc_in0"), sem("lo_bc_in1")]
        deg_onehots = sem("deg_onehots")
        deg_free = sem("deg_free")
        deg_done = sem("deg_done")
        deg_ready = sem("deg_ready")
        deg_rooted = sem("deg_rooted")
        dis_ready = sem("dis_ready")
        oht_ready = sem("oht_ready")
        looked_up = sem("looked_up")
        lookup_free = sem("lookup_free")
        src_free = sem("src_free")
        deg_lo = sem("deg_lo")
        weighted_ready = sem("weighted_ready")
        sums_done = sem("sums_done")
        mean_ready = sem("mean_ready")
        sq_done = sem("sq_done")
        var_ready = sem("var_ready")
        sd_ready = sem("sd_ready")
        norm_ready = sem("norm_ready")
        xhat_ready = sem("xhat_ready")
        node_w = sem("node_w")
        v_done = sem("v_done")
        v_copied = sem("v_copied")
        th_done = sem("th_done")
        th_bcast = sem("th_bcast")
        z_done = sem("z_done")
        z_ready = sem("z_ready")
        sig_ready = sem("sig_ready")

        S1_DEG = 0
        S1_ACC = 1

        N_CONSTS = 16

        with nc.Block() as block:
            @block.gpsimd
            def _(pool):
                pool.memset(XH[96:P, NT - 1, :], 0.0).then_inc(pads_set, 1)
                pool.wait_ge(pads_set, 1)
                pool.memset(dst_i[:, EC:NCH], PAD_INDEX).then_inc(pads_set, 1)
                pool.memset(src_i[:, EC:NCH], PAD_INDEX).then_inc(pads_set, 1)
                made = [0]

                def const(ins):
                    ins.then_inc(consts_set, 1)
                    made[0] += 1

                const(pool.iota(iota_lo, pattern=[[1, P], [0, GC]], base=0, channel_multiplier=0,
                                allow_small_or_imprecise_dtypes=True))
                const(pool.iota(iota_hi, pattern=[[1, NT], [0, GC]], base=0, channel_multiplier=0,
                                allow_small_or_imprecise_dtypes=True))
                const(pool.memset(ident[:, :], 0.0))
                const(pool.memset(identb[:, :], 0.0))
                const(pool.memset(upper[:, :], 1.0))
                const(pool.memset(onesb[:, :], 1.0))
                const(pool.memset(zerob[:, :], 0.0))
                const(pool.memset(rowmask[:, :], 1.0))
                const(pool.memset(cnt_in[:, :, :], 0.0))
                const(pool.iota(iota_p[:, :], pattern=[[0, 1]], base=0, channel_multiplier=1,
                                allow_small_or_imprecise_dtypes=True))
                const(pool.iota(iota16[:, :], pattern=[[1, E]], base=0, channel_multiplier=0,
                                allow_small_or_imprecise_dtypes=True))
                const(pool.iota(ecap[:, :], pattern=[[CAP, E]], base=0, channel_multiplier=0,
                                allow_small_or_imprecise_dtypes=True))
                pool.wait_ge(consts_set, made[0])
                for m in (ident, identb):
                    const(pool.affine_select(out=m[:, :], in_=m[:, :], compare_op=ALU.not_equal, fill=1.0,
                                             base=0, pattern=[[-1, P]], channel_multiplier=1))
                const(pool.affine_select(out=upper[:, :], in_=upper[:, :], compare_op=ALU.is_gt, fill=0.0,
                                         base=0, pattern=[[1, P]], channel_multiplier=-1))
                const(pool.affine_select(out=rowmask[:, :], in_=rowmask[:, :], compare_op=ALU.is_gt, fill=0.0,
                                         base=LAST, pattern=[[0, 1]], channel_multiplier=-1))
                assert made[0] == N_CONSTS

            @block.sync
            def _(sp):
                sp.wait_ge(pads_set, 3)
                for a, b in ((dst, dst_i), (src, src_i)):
                    sp.dma_start(b[:, 0:EC], a[0:EC * P].rearrange("(p c) -> p c", p=P)).then_inc(idx_in, 16)
                    sp.dma_start(b[0:ETAIL, EC:EC + 1],
                                 a[EC * P:EDGES].rearrange("(p c) -> p c", p=ETAIL)).then_inc(idx_in, 16)
                sp.dma_start(XH[:, 0:NT - 1, :],
                             x[0:(NT - 1) * P, :].rearrange("(t p) c -> p t c", p=P)).then_inc(x_loaded, 16)
                sp.dma_start(XH[0:LAST, NT - 1, :], x[(NT - 1) * P:N, :]).then_inc(x_loaded, 16)
                for e in range(EARLY):
                    load_expert(sp, e, weights_in)
                sp.wait_ge(loT_copied, 2)
                sp.dma_start(lo_rows[0:(BLK - 1) * P, :].rearrange("(b q) m -> q b m", q=P),
                             loT[:, 0:BLK - 1, :]).then_inc(lo_stored, 16)
                sp.dma_start(lo_rows[(BLK - 1) * P:NCH, :],
                             loT[0:NCH - (BLK - 1) * P, BLK - 1, :]).then_inc(lo_stored, 16)
                sp.wait_ge(lo_stored, 32)

                def load_lo(g, u):
                    sp.dma_start(lo_bc[:, u, :],
                                 lo_rows[ds(g * GC, GC), :].rearrange("c m -> (c m)").partition_broadcast(P)
                                 ).then_inc(lo_bc_in[u], 16)
                sp.wait_ge(idx_split, 4)
                load_lo(0, 0)
                load_lo(1, 1)
                with sp.Fori(1, NG // 2) as i:
                    for u in range(2):
                        sp.wait_ge(oht_ready, 2 * i + (u - 1))
                        load_lo(2 * i + u, u)
                sp.wait_ge(src_free, NG + 2)
                sp.dma_start(gW2_sb[0:HID, :], gW2).then_inc(gb2_in, 16)
                sp.dma_start(gb2_bc, gb2.partition_broadcast(P)).then_inc(gb2_in, 16)

            @block.scalar
            def _(act):
                act.dma_start(gw_sb[:, :, :], gate_w.rearrange("(p k) e -> p k e", k=2)).then_inc(small_in, 16)
                act.dma_start(gateb_bc[:, :], gate_b.partition_broadcast(P)).then_inc(small_in, 16)
                act.dma_start(gW1_sb[:, :, :], gW1.rearrange("(k p) h -> p k h", p=P)).then_inc(small_in, 16)
                act.dma_start(gb1_col[:, :], gb1.rearrange("(p o) -> p o", o=1)).then_inc(small_in, 16)
                act.dma_start(b1T[:, :, :], b1.rearrange("e (p j) -> p e j", j=4)).then_inc(small_in, 16)
                act.dma_start(b2_sb[:, :], b2).then_inc(small_in, 16)
                act.wait_ge(lo_turned, 1)
                turned = PS[:, 2, :].bitcast(bf16).rearrange("p (b m) -> p b m", m=P)
                act.activation(loT[:, 0:BLK - 1, :], turned[:, 0:BLK - 1, :], ACT.Copy).then_inc(loT_copied, 1)
                act.activation(loT[0:64, BLK - 1, :], turned[0:64, BLK - 1, :], ACT.Copy).then_inc(loT_copied, 1)
                act.wait_ge(x_loaded, 32)
                link = linker(act, act_step)
                with act.Fori(0, NT) as t:
                    link.rebase(t)
                    link(nc.scalar.activation(junk, XH[:, ds(t, 1), :].rearrange("p o c -> p (o c)"), ACT.Copy,
                                              accum_out=lnsum[:, ds(t, 1)]))
                act.activation(sd[:, :], lnsum, ACT.Copy).then_inc(sums_done, 1)
                act.wait_ge(deg_ready, 1)
                act.activation(tmpa[:, :], deg[:, :], ACT.Sqrt).then_inc(deg_rooted, 1)
                act.wait_ge(mean_ready, 1)
                with act.Fori(0, NT) as t:
                    link.rebase(t + NT)
                    link(nc.scalar.activation(junk, XH[:, ds(t, 1), :].rearrange("p o c -> p (o c)"), ACT.Square,
                                              bias=nmean[:, ds(t, 1)], accum_out=lnsq[:, ds(t, 1)]))
                act.activation(sd[:, :], lnsq, ACT.Copy).then_inc(sq_done, 1)
                act.wait_ge(var_ready, 1)
                act.activation(sd[:, :], lnsq[:, :], ACT.Sqrt).then_inc(sd_ready, 1)
                act.wait_ge(norm_ready, 1)
                with act.Fori(0, NT) as t:
                    row = XH[:, ds(t, 1), :].rearrange("p o c -> p (o c)")
                    nc.scalar.activation(row, row, ACT.Identity, bias=nmr[:, ds(t, 1)],
                                         scale=rstd[:, ds(t, 1)]).then_inc(xhat_ready, 1)
                act.wait_ge(v_done, 1)
                act.activation(vcol[:, :], PS[:, 2, 0:2], ACT.Copy).then_inc(v_copied, 1)
                act.wait_ge(th_done, 1)
                act.wait_ge(small_in, 96)
                act.activation(th[:, :], PS[0:HID, 3, 0:1], ACT.Relu, bias=gb1_col[:, :],
                               scale=1.0 / N).then_inc(th_bcast, 1)
                act.wait_ge(th_bcast, 1)
                act.activation(th_bc[0:HID, :], th[:, :].to_broadcast([HID, P]), ACT.Copy).then_inc(th_bcast, 1)
                act.wait_ge(z_ready, 1)
                act.activation(theta, gb2_bc, ACT.Sigmoid).then_inc(sig_ready, 1)

            @block.tensor
            def _(pe):
                pe.wait_ge(consts_set, N_CONSTS)
                pe.wait_ge(idx_split, 1)
                turned = PS[:, 2, :].bitcast(bf16).rearrange("p (b m) -> p b m", m=P)
                for b in range(BLK):
                    cols = min(P, NCH - b * P)
                    last = nc.tensor.transpose(turned[0:cols, b, :], dlo[:, b * P:b * P + cols], identb[:, :])
                last.then_inc(lo_turned, 1)
                nc.tensor.matmul(PS[:, S1_DEG, 0:NT], zerob[:, :], zerob[:, 0:NT], start=True, stop=False)
                pe.sem_inc(deg_free, 2)
                with pe.Fori(0, NG // 2) as i:
                    for u in range(2):
                        pe.wait_ge(deg_onehots, 2 * i + (u + 1))
                        for c in range(GC):
                            last = nc.tensor.matmul(PS[:, S1_DEG, 0:NT], oh_lo[:, u, :, c], oh_hi[:, u, :, c],
                                                    start=False, stop=False)
                        last.then_inc(deg_free, 1)
                nc.tensor.matmul(PS[:, S1_DEG, 0:NT], zerob[:, :], zerob[:, 0:NT], start=False,
                                 stop=True).then_inc(deg_done, 1)
                nc.tensor.matmul(PS[:, S1_ACC, 0:2 * NT], zerob[:, :], zerob[:, 0:2 * NT], start=True, stop=False)
                pe.wait_ge(dis_ready, 1)
                pe.wait_ge(loT_copied, 2)
                HC = GC // 2

                def lookup(g, u):
                    pe.wait_ge(oht_ready, g + 1)
                    for h in range(2):
                        pe.wait_ge(lookup_free, 2 * g + (h + 1))
                        for c in range(HC):
                            o = PS[:, 2 + 2 * h + c // 8, (c % 8) * NT:(c % 8 + 1) * NT]
                            lhs = oh_t[:, u, (h * HC + c) * P:(h * HC + c + 1) * P]
                            for k in range(3):
                                last = nc.tensor.matmul(o, lhs, dis3[:, k, :], start=(k == 0), stop=(k == 2))
                        last.then_inc(looked_up, 1)

                def scatter(g, u):
                    pe.wait_ge(weighted_ready, g + 1)
                    for c in range(GC):
                        last = nc.tensor.matmul(PS[:, S1_ACC, 0:2 * NT], oh_lo[:, u, :, c],
                                                weighted[:, u, :, :, c], start=False, stop=False)
                    last.then_inc(src_free, 1)

                lookup(0, 0)
                with pe.Fori(0, NG // 2 - 1) as i:
                    for u in range(2):
                        lookup(2 * i + (u + 1), 1 - u)
                        scatter(2 * i + u, u)
                lookup(NG - 1, 1)
                scatter(NG - 2, 0)
                scatter(NG - 1, 1)
                nc.tensor.matmul(PS[:, S1_ACC, 0:2 * NT], zerob[:, :], zerob[:, 0:2 * NT], start=False,
                                 stop=True).then_inc(deg_done, 1)
                pe.wait_ge(node_w, 1)
                pe.wait_ge(xhat_ready, NT)
                for k in range(2):
                    for t in range(NT):
                        last = nc.tensor.matmul(PS[:, 2, k:k + 1], XH[:, t, k * P:(k + 1) * P], wts[:, t:t + 1],
                                                start=(t == 0), stop=(t == NT - 1))
                last.then_inc(v_done, 1)
                pe.wait_ge(v_copied, 1)
                pe.wait_ge(small_in, 96)
                for k in range(2):
                    last = nc.tensor.matmul(PS[0:HID, 3, 0:1], gW1_sb[:, k, :], vcol[:, k:k + 1],
                                            start=(k == 0), stop=(k == 1))
                last.then_inc(th_done, 1)
                pe.wait_ge(th_bcast, 2)
                pe.wait_ge(gb2_in, 32)
                for q in range(2):
                    last = nc.tensor.matmul(PS[:, 4 + q, :], th_bc[0:HID, :], gW2_sb[0:HID, q * 512:(q + 1) * 512],
                                            start=True, stop=True)
                last.then_inc(z_done, 1)

            @block.vector
            def _(dve):
                link = linker(dve, dve_step)
                dve.wait_ge(idx_in, 64)
                dve.wait_ge(consts_set, N_CONSTS)
                for raw, lo, hi in ((dst_i, dlo, dhi), (src_i, slo, shi)):
                    if raw is src_i:
                        dve.wait_ge(idx_split, 2)
                    link(nc.vector.tensor_scalar(lo_i, raw, P - 1, None, ALU.bitwise_and))
                    nc.vector.tensor_copy(lo, lo_i).then_inc(idx_split, 1)
                    link(nc.vector.tensor_scalar(hi_i, raw, LO_BITS, None, ALU.logical_shift_right))
                    nc.vector.tensor_copy(hi, hi_i).then_inc(idx_split, 1)
                dve.wait_ge(idx_split, 4)

                def onehot(into, part, values, g, size):
                    return nc.vector.tensor_tensor(into, part[:, ds(g * GC, GC)].unsqueeze(1)
                                                   .to_broadcast([P, size, GC]), values, ALU.is_equal)

                with dve.Fori(0, NG // 2) as i:
                    for u in range(2):
                        g = 2 * i + u
                        dve.wait_ge(deg_free, g + 1)
                        onehot(oh_lo[:, u], dlo, iota_lo, g, P).then_inc(deg_lo, 1)
                        onehot(oh_hi[:, u], dhi, iota_hi, g, NT).then_inc(deg_onehots, 1)
                dve.wait_ge(sums_done, 1)
                nc.vector.tensor_scalar(nmean[:, :], lnsum[:, :], -1.0 / C, None, ALU.mult).then_inc(mean_ready, 1)
                dve.wait_ge(deg_done, 1)
                nc.vector.tensor_scalar(deg[:, :], PS[:, S1_DEG, 0:NT], 1.0, None, ALU.add).then_inc(deg_ready, 1)
                dve.wait_ge(deg_rooted, 1)
                link(nc.vector.reciprocal(dis[:, :], tmpa[:, :]))
                link(nc.vector.tensor_tensor(tmpb[:, :], dis[:, :], dis[:, :], ALU.mult))
                link(nc.vector.tensor_tensor(tmpb[:, :], tmpb[:, :], deg[:, :], ALU.mult))
                link(nc.vector.tensor_scalar(tmpb[:, :], tmpb[:, :], -0.5, 1.5, ALU.mult, ALU.add))
                link(nc.vector.tensor_tensor(dis[:, :], dis[:, :], tmpb[:, :], ALU.mult))
                link(nc.vector.tensor_copy(dis3[:, 0, :], dis[:, :]))
                link(nc.vector.tensor_tensor(tmpa[:, :], dis[:, :], dis3[:, 0, :], ALU.subtract))
                link(nc.vector.tensor_copy(dis3[:, 1, :], tmpa[:, :]))
                link(nc.vector.tensor_tensor(tmpb[:, :], tmpa[:, :], dis3[:, 1, :], ALU.subtract))
                nc.vector.tensor_copy(dis3[:, 2, :], tmpb[:, :]).then_inc(dis_ready, 1)
                dve.wait_ge(deg_free, NG + 2)
                dve.sem_inc(lookup_free, 2)
                dve.sem_inc(src_free, 2)
                before = link.state[1]
                PER = 2 * 12
                def select_lo(g, u, turn):
                    dve.wait_ge(lo_bc_in[u], 16 * turn + 16)
                    nc.vector.tensor_scalar(oh_t[:, u, :], lo_bc[:, u, :], iota_p[:, :], None,
                                            ALU.is_equal).then_inc(oht_ready, 1)

                def lookup_pair(i, base, last=False):
                    link.rebase(i * PER + base)
                    for u in range(2):
                        g = 2 * i + u
                        dve.wait_ge(src_free, g + 1)
                        link(onehot(oh_hi[:, u], dhi, iota_hi, g, NT))
                        link(onehot(oh_lo[:, u], slo, iota_lo, g, P))
                        link(onehot(oh_src[:, u], shi, iota_hi, g, NT))
                        if not (last and u == 1):
                            select_lo(g + 1, 1 - u, i + u)
                        for h in range(2):
                            dve.wait_ge(looked_up, 2 * g + (h + 1))
                            rows = PS[:, 2 + 2 * h:4 + 2 * h, 0:8 * NT]
                            hot = oh_hi[:, u].rearrange("p t c -> p c t")[:, h * (GC // 2):(h + 1) * (GC // 2), :]
                            for q in range(2):
                                ins = nc.vector.tensor_tensor(
                                    picked[:, h * 16 + q * 8:h * 16 + q * 8 + 8, :],
                                    PS[:, 2 + 2 * h + q, 0:8 * NT].rearrange("p (c t) -> p c t", t=NT),
                                    hot[:, q * 8:q * 8 + 8, :], ALU.mult)
                                link(ins)
                            dve.sem_inc(lookup_free, 1)
                        link(nc.vector.tensor_reduce(g_val, picked, AX.X, ALU.add))
                        link(nc.vector.tensor_copy(g_two[:, 0, :], g_val))
                        link(nc.vector.tensor_tensor(g_rest, g_val, g_two[:, 0, :], ALU.subtract))
                        link(nc.vector.tensor_scalar(g_two[:, 1, :], g_rest, 2048.0, None, ALU.mult))
                        for k in range(2):
                            ins = nc.vector.tensor_tensor(weighted[:, u, k], oh_src[:, u],
                                                          g_two[:, k, :].unsqueeze(1).to_broadcast([P, NT, GC]),
                                                          ALU.mult)
                            if k == 0:
                                link(ins)
                            else:
                                ins.then_inc(weighted_ready, 1)
                    assert link.state[1] == PER, link.state

                select_lo(0, 0, 0)
                HALF = NG // 4
                with dve.Fori(0, HALF) as i:
                    lookup_pair(i, before)
                link.rebase(before + PER * HALF)
                dve.wait_ge(sq_done, 1)
                nc.vector.tensor_scalar(lnsq[:, :], lnsq[:, :], 1.0 / C, EPS, ALU.mult, ALU.add).then_inc(var_ready, 1)
                dve.wait_ge(sd_ready, 1)
                link(nc.vector.reciprocal(rstd[:, :], sd[:, :]))
                dve.wait_ge(mean_ready, 1)
                nc.vector.tensor_tensor(nmr[:, :], nmean[:, :], rstd[:, :], ALU.mult).then_inc(norm_ready, 1)
                with dve.Fori(HALF, NG // 2 - 1) as i:
                    lookup_pair(i, before + 1)
                lookup_pair(NG // 2 - 1, before + 1, last=True)
                before += 1
                dve.wait_ge(deg_done, 2)
                link.rebase(before + PER * (NG // 2))
                link(nc.vector.tensor_scalar(tmpa[:, :], PS[:, S1_ACC, NT:2 * NT], 1.0 / 2048, None, ALU.mult))
                link(nc.vector.tensor_tensor(tmpa[:, :], PS[:, S1_ACC, 0:NT], tmpa[:, :], ALU.add))
                link(nc.vector.tensor_tensor(tmpa[:, :], tmpa[:, :], dis[:, :], ALU.add))
                nc.vector.tensor_tensor(wts[:, :], tmpa[:, :], dis[:, :], ALU.mult).then_inc(node_w, 1)
                dve.wait_ge(z_done, 1)
                for q in range(2):
                    ins = nc.vector.tensor_tensor(gb2_bc[:, q * 512:(q + 1) * 512], PS[:, 4 + q, :],
                                                  gb2_bc[:, q * 512:(q + 1) * 512], ALU.add)
                    link(ins)
                dve.sem_inc(z_ready, 1)
                dve.wait_ge(sig_ready, 1)
                link(nc.vector.tensor_scalar(theta, theta, 2.0, -1.0, ALU.mult, ALU.add))
                th4 = theta.rearrange("p (c j) -> p j c", j=4)
                link(nc.vector.tensor_scalar(coef[:, 0, :], th4[:, 0, :], 1.0, 1.0, ALU.mult, ALU.add))
                link(nc.vector.tensor_copy(coef[:, 1, :], th4[:, 1, :]))
                link(nc.vector.tensor_scalar(coef[:, 2:4, :], th4[:, 2:4, :], 0.5, None, ALU.mult))

        xin_in = [sem("xin_in0"), sem("xin_in1")]
        xin_free = sem("xin_free")
        stats_taken = sem("stats_taken")
        dve2 = sem("dve2")
        var2 = sem("var2")
        sd2 = sem("sd2")
        norm2 = sem("norm2")
        xn_ready = sem("xn_ready")
        xn_sent = [sem("xn_sent0"), sem("xn_sent1")]
        turned2 = sem("turned2")
        turned2_read = sem("turned2_read")
        logits_done = sem("logits_done")
        logits_read = sem("logits_read")
        counted = sem("counted")
        prefixed = sem("prefixed")
        slots_ready = sem("slots_ready")
        pads_ready = sem("pads_ready")
        pads_in = sem("pads_in")
        tab_ready = sem("tab_ready")
        tab_turned = sem("tab_turned")
        d_ready = sem("d_ready")
        zrows_set = sem("zrows_set")
        rstd2 = sem("rstd2")
        masked = sem("masked")
        e_ready = sem("e_ready")

        def pairs(eng, body):
            for u in range(2):
                body(u, 0, u, False)
            with eng.Fori(1, NGT // 2) as i:
                for u in range(2):
                    body(2 * i + u, i, u, False)
            body(NGT - 1, NGT // 2, 0, True)

        with nc.Block() as block:
            @block.sync
            def _(sp):
                for e in range(EARLY, MIDDLE):
                    load_expert(sp, e, weights_in)

                def load_x(g, i, u, last):
                    sp.wait_ge(xin_free, g + 1)
                    head = (GT - 1) * P
                    rows = LAST if last else P
                    sp.dma_start(x_in[:, u, 0:GT - 1, :],
                                 x[ds(g * (GT * P), head), :].rearrange("(t p) c -> p t c", p=P)
                                 ).then_inc(xin_in[u], 16)
                    sp.dma_start(x_in[0:rows, u, GT - 1, :], x[ds(g * (GT * P) + head, rows), :]
                                 ).then_inc(xin_in[u], 16)
                pairs(sp, load_x)
                sp.wait_ge(pads_ready, 1)
                sp.wait_ge(zrows_set, 1)
                with sp.Fori(0, E // 2) as e:
                    row = sp.value_load(pad_i[0:1, ds(e, 1)], min_val=0, max_val=XROWS - P)
                    sp.dma_start(xs[ds(row, P), :], zrows).then_inc(pads_in, 16)
                for u in range(2):
                    sp.wait_ge(xn_sent[u], 16 * 2 * GT * (NGT - NGT // 2 if u == 0 else NGT // 2))
                sp.wait_ge(pads_in, 16 * E)

            @block.gpsimd
            def _(pool):
                def send(g, i, u, last):
                    pool.wait_ge(slots_ready, g + 1)
                    pool.sem_inc(wait_mark, 1)
                    for j in range(GT):
                        rows = LAST if last and j == GT - 1 else P
                        for k in range(2):
                            nc.gpsimd.indirect_dma_start(
                                out=xs[:, :], out_offset=bass.IndirectOffsetOnAxis(ap=slot_i[0:rows, u, j, k:k + 1], axis=0),
                                in_=xn[0:rows, u, j, :], in_offset=None).then_inc(xn_sent[u], 16)

                nc.gpsimd.memset(zrows, 0.0).then_inc(zrows_set, 1)
                pairs(pool, send)

            @block.scalar
            def _(act):
                def normalise(g, i, u, last):
                    act.wait_ge(var2, g + 1)
                    act.activation(sd[:, ds(g * GT, GT)], tmpa[:, ds(g * GT, GT)], ACT.Sqrt).then_inc(sd2, 1)
                    act.wait_ge(norm2, g + 1)
                    wait_past(act, xn_sent[u], (16 * 2 * GT) * i)
                    for j in range(GT):
                        row = XH[:, ds(g * GT + j, 1), :].rearrange("p o c -> p (o c)")
                        nc.scalar.activation(xn[:, u, j, :], row, ACT.Identity, bias=nmr[:, ds(g * GT + j, 1)],
                                             scale=rstd[:, ds(g * GT + j, 1)]).then_inc(xn_ready, 1)
                    wait_past(act, logits_done, g + 0)
                    for b in range(4):
                        n = 2 if b < 3 else 1
                        act.wait_ge(turned2, 4 * g + (b + 1))
                        act.activation(xnT[:, 2 * b:2 * b + n], PS[:, b, 0:n * C].rearrange("p (j k m) -> p j k m", j=n, k=2),
                                       ACT.Copy).then_inc(turned2_read, 1)
                pairs(act, normalise)
                act.wait_ge(pads_ready, 1)
                act.wait_ge(zrows_set, 1)
                with act.Fori(E // 2, E) as e:
                    row = act.value_load(pad_i[0:1, ds(e, 1)], min_val=0, max_val=XROWS - P)
                    act.dma_start(xs[ds(row, P), :], zrows).then_inc(pads_in, 16)
                act.wait_ge(d_ready, 1)
                act.activation(sd[:, :], tmpa[:, :], ACT.Exp).then_inc(e_ready, 1)

            @block.tensor
            def _(pe):
                def gate(g, i, u, last):
                    for b in range(4):
                        n = 2 if b < 3 else 1
                        pe.wait_ge(xn_ready, GT * g + (2 * b + n))
                        wait_past(pe, turned2_read, 4 * g + 0)
                        for j in range(n):
                            for k in range(2):
                                last_ins = nc.tensor.transpose(
                                    PS[:, b, j * C + k * P:j * C + (k + 1) * P],
                                    xn[:, u, 2 * b + j, :].rearrange("p (c k) -> p k c", k=2)[:, k, :], ident[:, :])
                        last_ins.then_inc(turned2, 1)
                    pe.wait_ge(turned2_read, 4 * g + 4)
                    wait_past(pe, logits_read, g + 0)
                    for j in range(GT):
                        for k in range(2):
                            last_ins = nc.tensor.matmul(PS[:, 4, j * E:(j + 1) * E], xnT[:, j, k, :], gw_sb[:, k, :],
                                                        start=(k == 0), stop=(k == 1))
                    last_ins.then_inc(logits_done, 1)
                    pe.wait_ge(counted, g + 1)
                    s = cnt_in[:, :, :].rearrange("p j e -> p (j e)")
                    nc.tensor.matmul(PS[:, 5, 0:(GT + 1) * E], upper[:, :], s, start=True, stop=False)
                    for j in range(GT):
                        o = PS[:, 5, (j + 1) * E:(GT + 1) * E].rearrange("p (j e) -> p j e", e=E)
                        last_ins = nc.tensor.matmul(o, onesb[:, :], cnt_in[:, j:j + 1, :].to_broadcast([P, GT - j, E]),
                                                    start=False, stop=(j == GT - 1))
                    last_ins.then_inc(prefixed, 1)
                pairs(pe, gate)
                pe.wait_ge(tab_ready, 1)
                nc.tensor.transpose(PS[0:1, 6, 0:P], et[:, 0:1], ident[:, :])
                nc.tensor.transpose(PS[0:1, 6, P:2 * P], et[:, 1:2], ident[:, :]).then_inc(tab_turned, 1)

            @block.vector
            def _(dve):
                link = linker(dve, dve2)
                dve.sem_inc(xin_free, 2)
                link(nc.vector.tensor_copy(carry[:, :], ecap[:, :]))
                A_STEPS, B_STEPS = 6 + 2, 3 + 1 + 2 + 2 + 4

                def affine(g, i, u):
                    rows = XH[:, ds(g * GT, GT), :]
                    cb = [coef[:, q, :].unsqueeze(1).to_broadcast([P, GT, C]) for q in range(4)]
                    link(nc.vector.tensor_tensor(branch, rows, cb[0], ALU.mult))
                    link(nc.vector.tensor_tensor(branch, branch, cb[2], ALU.add))
                    link(nc.vector.tensor_tensor(rows, rows, cb[1], ALU.mult))
                    link(nc.vector.tensor_tensor(rows, rows, cb[3], ALU.add))
                    link(nc.vector.tensor_tensor(rows, rows, branch, ALU.max))
                    dve.wait_ge(xin_in[u], 32 * i + 32)
                    link(nc.vector.tensor_tensor(rows, rows, x_in[:, u], ALU.add))
                    dve.sem_inc(xin_free, 1)
                    for j in range(GT):
                        ins = nc.vector.bn_stats(st2[:, j, :],
                                                 XH[:, ds(g * GT + j, 1), :].rearrange("p o c -> p (o c)"))
                    link(ins)
                    dve.sem_inc(stats_taken, 1)
                    for j in range(GT):
                        ins = nc.vector.bn_aggr(mv2[:, j, :], st2[:, j, :])
                    link(ins)
                    nc.vector.tensor_scalar(tmpa[:, ds(g * GT, GT)], mv2[:, :, 1],
                                            EPS, None, ALU.add).then_inc(var2, 1)

                def scale(g):
                    dve.wait_ge(sd2, g + 1)
                    nc.vector.reciprocal(rstd[:, ds(g * GT, GT)], sd[:, ds(g * GT, GT)]).then_inc(rstd2, 1)
                    dve.wait_ge(rstd2, g + 1)
                    nc.vector.scalar_tensor_tensor(nmr[:, ds(g * GT, GT)],
                                                   mv2[:, :, 0], -1.0,
                                                   rstd[:, ds(g * GT, GT)], ALU.mult, ALU.mult).then_inc(norm2, 1)

                def route(g, i, u, last=False):
                    dve.wait_ge(logits_done, g + 1)
                    link(nc.vector.tensor_tensor(logit[:, :, :], PS[:, 4, 0:GT * E].rearrange("p (j e) -> p j e", e=E),
                                                 gateb_bc[:, :].unsqueeze(1).to_broadcast([P, GT, E]), ALU.add))
                    dve.sem_inc(logits_read, 1)
                    for j in range(GT):
                        ins = nc.vector.max(top[:, j, :], logit[:, j, :])
                    link(ins)
                    nc.vector.tensor_scalar(TOPV[:, ds(g * GT, GT), :], top[:, :, 0:2], 1.0, None, ALU.mult)
                    for j in range(GT):
                        ins = nc.vector.max_index(topi[:, j, :], top[:, j, :], logit[:, j, :])
                    link(ins)
                    link(nc.vector.tensor_scalar(IDX[:, ds(g * GT, GT), :], topi[:, :, 0:2], 1.0, None, ALU.mult))
                    for k in range(2):
                        link(nc.vector.tensor_tensor(
                            oh[:, k], iota16[:, :].unsqueeze(1).to_broadcast([P, GT, E]),
                            IDX[:, ds(g * GT, GT), k:k + 1].to_broadcast([P, GT, E]), ALU.is_equal))
                    if last:
                        for k in range(2):
                            nc.vector.tensor_scalar(oh[:, k, GT - 1, :], oh[:, k, GT - 1, :], rowmask[:, :], None,
                                                    ALU.mult).then_inc(masked, 1)
                        dve.wait_ge(masked, 2)
                    nc.vector.tensor_tensor(cnt_in[:, 0:GT, :], oh[:, 0], oh[:, 1], ALU.add).then_inc(counted, 1)
                    dve.wait_ge(prefixed, g + 1)
                    link(nc.vector.tensor_tensor(posq[:, :, :], PS[:, 5, 0:GT * E].rearrange("p (j e) -> p j e", e=E),
                                                 carry[:, :].unsqueeze(1).to_broadcast([P, GT, E]), ALU.add))
                    link(nc.vector.tensor_tensor(carry[:, :], PS[:, 5, GT * E:(GT + 1) * E], carry[:, :], ALU.add))
                    for k in range(2):
                        link(nc.vector.tensor_tensor(prodq[:, :, :], oh[:, k], posq[:, :, :], ALU.mult))
                        link(nc.vector.tensor_reduce(SLOT[:, ds(g * GT, GT), k:k + 1].rearrange("p t o -> p (t o)"),
                                                     prodq[:, :, :], AX.X, ALU.add))
                    wait_past(dve, xn_sent[u], (16 * 2 * GT) * i)
                    nc.vector.tensor_scalar(slot_i[:, u], SLOT[:, ds(g * GT, GT), :], 1.0, None, ALU.mult).then_inc(slots_ready, 1)

                affine(0, 0, 0)
                scale(0)
                start = link.state[1]
                def pair(i):
                    link.rebase(i * (2 * (A_STEPS + B_STEPS)) + start)
                    affine(2 * i + 1, i, 1)
                    route(2 * i, i, 0)
                    scale(2 * i + 1)
                    affine(2 * i + 2, i + 1, 0)
                    route(2 * i + 1, i, 1)
                    scale(2 * i + 2)
                    assert link.state[1] == 2 * (A_STEPS + B_STEPS), link.state
                pair(0)
                with dve.Fori(1, NGT // 2) as i:
                    pair(i)
                link.rebase(start + (NGT // 2) * 2 * (A_STEPS + B_STEPS))
                route(NGT - 1, NGT // 2, 0, True)
                nc.vector.tensor_copy(pad_i[:, :], carry[0:1, :]).then_inc(pads_ready, 1)
                link(nc.vector.tensor_tensor(p16[:, :], carry[:, :], ecap[:, :], ALU.subtract))
                link(nc.vector.tensor_scalar(p16[:, :], p16[:, :], float(P - 1), None, ALU.add))
                link(nc.vector.tensor_copy(cnti[:, :], p16[:, :]))
                link(nc.vector.tensor_scalar(cnti[:, :], cnti[:, :], LO_BITS, None, ALU.logical_shift_right))
                link(nc.vector.tensor_copy(nt16[:, :], cnti[:, :]))
                link(nc.vector.tensor_copy(cum[:, 0, :], nt16[:, :]))
                cur = 0
                for s in (1, 2, 4, 8):
                    link(nc.vector.tensor_copy(cum[:, 1 - cur, 0:s], cum[:, cur, 0:s]))
                    link(nc.vector.tensor_tensor(cum[:, 1 - cur, s:E], cum[:, cur, s:E], cum[:, cur, 0:E - s], ALU.add))
                    cur = 1 - cur
                link(nc.vector.tensor_scalar(fin16[:, :], cum[:, cur, :], iota_p[:, :], None, ALU.is_le))
                link(nc.vector.tensor_reduce(et[:, 0:1], fin16[:, :], AX.X, ALU.add))
                link(nc.vector.tensor_tensor(p16[:, :], fin16[:, :], nt16[:, :], ALU.mult))
                link(nc.vector.tensor_reduce(et[:, 2:3], p16[:, :], AX.X, ALU.add))
                link(nc.vector.tensor_tensor(et[:, 2:3], iota_p[:, :], et[:, 2:3], ALU.subtract))
                link(nc.vector.tensor_scalar(et[:, 3:4], et[:, 0:1], float(CAP), None, ALU.mult))
                link(nc.vector.scalar_tensor_tensor(et[:, 1:2], et[:, 2:3], float(P), et[:, 3:4], ALU.mult, ALU.add))
                link(nc.vector.tensor_scalar(et[:, 3:4], et[:, 0:1], float(E) - 0.5, None, ALU.is_lt))
                link(nc.vector.tensor_tensor(et[:, 1:2], et[:, 1:2], et[:, 3:4], ALU.mult))
                nc.vector.tensor_scalar(et[:, 0:1], et[:, 0:1], float(E - 1), None, ALU.min).then_inc(tab_ready, 1)
                dve.wait_ge(tab_turned, 1)
                link(nc.vector.tensor_copy(tile_e[:, :], PS[0:1, 6, 0:P]))
                link(nc.vector.tensor_copy(tile_r[:, :], PS[0:1, 6, P:2 * P]))
                link(nc.vector.tensor_tensor(dbase[:, :], cum[:, cur, :], nt16[:, :], ALU.subtract))
                link(nc.vector.tensor_scalar(dbase[:, :], dbase[:, :], float(P), None, ALU.mult))
                link(nc.vector.tensor_tensor(dbase[:, :], dbase[:, :], ecap[:, :], ALU.subtract))
                nc.vector.tensor_tensor(tmpa[:, :], TOPV[:, :, 1:2].rearrange("p t o -> p (t o)"),
                                        TOPV[:, :, 0:1].rearrange("p t o -> p (t o)"), ALU.subtract).then_inc(d_ready, 1)
                dve.wait_ge(e_ready, 1)
                link(nc.vector.tensor_scalar(tmpb[:, :], sd[:, :], 1.0, None, ALU.add))
                link(nc.vector.reciprocal(WT[:, 0, :], tmpb[:, :]))
                link(nc.vector.tensor_tensor(WT[:, 1, :], WT[:, 0, :], sd[:, :], ALU.mult))

        x3_in = [sem("x3_in0"), sem("x3_in1")]
        x_turned = sem("x_turned")
        xt_copied = sem("xt_copied")
        mm1_done = sem("mm1_done")
        h_copied = sem("h_copied")
        h_turned = sem("h_turned")
        relu_act = sem("relu_act")
        relu_dve = sem("relu_dve")
        mm2_done = sem("mm2_done")
        o_copied = sem("o_copied")
        o_sent = [sem("o_sent0"), sem("o_sent1")]
        pool3 = sem("pool3")

        with nc.Block() as block:
            def odd_even(eng, body):
                body(1, 1, 0)
                body(2, 0, 1)
                with eng.Fori(1, (MT - 2) // 2) as i:
                    body(2 * i + 1, 1, i)
                    body(2 * i + 2, 0, i + 1)

            @block.sync
            def _(sp):
                def load(t, u):
                    row = sp.value_load(tile_r[0:1, ds(t, 1)], min_val=0, max_val=XROWS - P)
                    sp.dma_start(X3[:, u, :], xs[ds(row, P), :]).then_inc(x3_in[u], 16)

                def store(t, u):
                    sp.wait_ge(o_copied, t + 3)
                    sp.dma_start(ys[ds(t * P, P), :], O3[:, u, :]).then_inc(o_sent[u], 16)

                load(0, 0)
                load(1, 1)
                sp.wait_ge(x_turned, 1)
                load(2, 0)
                sp.wait_ge(x_turned, 2)
                load(3, 1)
                store(0, 0)
                with sp.Fori(1, MT // 2 - 1) as i:
                    for u in range(2):
                        sp.wait_ge(x_turned, 2 * i + (u + 1))
                        load(2 * i + (u + 2), u)
                        store(2 * i + (u - 1), 1 - u)
                store(MT - 3, 1)
                store(MT - 2, 0)
                store(MT - 1, 1)
                for u in range(2):
                    sp.wait_ge(o_sent[u], 16 * (MT // 2))

            @block.tensor
            def _(pe):
                def turn_x(t, u, half):
                    pe.wait_ge(x3_in[u], 16 * half + 16)
                    cols = X3[:, u, :].rearrange("p (c k) -> p k c", k=2)
                    for k in range(2):
                        last = nc.tensor.transpose(PS[:, u, k * P:(k + 1) * P], cols[:, k, :], ident[:, :])
                    last.then_inc(x_turned, 1)

                def up(t, u, e):
                    pe.wait_ge(xt_copied, t + 1)
                    pe.wait_ge(experts_ready, e + 1)
                    for k in range(2):
                        last = nc.tensor.matmul(PS[:, 2 + u, :], XT3[:, u, k, :], wt1(e * WCOLS, k),
                                                start=(k == 0), stop=(k == 1))
                    last.then_inc(mm1_done, 1)

                def turn_h(t, u):
                    pe.wait_ge(h_copied, t + 1)
                    cols = H3[:, u, :].rearrange("p (c j) -> p j c", j=4)
                    for j in range(4):
                        last = nc.tensor.transpose(PS[:, 4 + j // 2, (j % 2) * P:(j % 2 + 1) * P], cols[:, j, :], ident[:, :])
                    last.then_inc(h_turned, 1)

                def down(t, u, e):
                    pe.wait_ge(relu_act, t + 1)
                    pe.wait_ge(relu_dve, t + 1)
                    pe.wait_ge(o_copied, t + 1)
                    for j in range(4):
                        last = nc.tensor.matmul(PS[:, 6 + u, 0:C], HT3[:, u, j, :], wt2(e * WCOLS, j),
                                                start=(j == 0), stop=(j == 3))
                    last.then_inc(mm2_done, 1)

                def expert_of(t):
                    return pe.value_load(tile_e[0:1, ds(t, 1)], min_val=0, max_val=E - 1)

                pe.sem_inc(o_copied, 2)
                pe.wait_ge(weights_in, 32 * MIDDLE)
                pe.sem_inc(experts_ready, MIDDLE)
                turn_x(0, 0, 0)
                turn_x(1, 1, 0)
                up(0, 0, expert_of(0))
                turn_h(0, 0)

                def step(t, u, i, cols, cols_before):
                    wait_past(pe, h_copied, t - 1)
                    up(t, u, cols)
                    pe.wait_ge(xt_copied, t + 0)
                    turn_x(t + 1, 1 - u, i + 1 if u == 1 else i)
                    down(t - 1, 1 - u, cols_before)
                    turn_h(t, u)

                def pair(i):
                    c = [expert_of(2 * i + n) for n in range(3)]
                    step(2 * i + 1, 1, i, c[1], c[0])
                    step(2 * i + 2, 0, i + 1, c[2], c[1])
                pair(0)
                with pe.Fori(1, (MT - 2) // 2) as i:
                    pair(i)
                pe.wait_ge(h_copied, MT - 2)
                up(MT - 1, 1, expert_of(MT - 1))
                down(MT - 2, 0, expert_of(MT - 2))
                turn_h(MT - 1, 1)
                down(MT - 1, 1, expert_of(MT - 1))

            @block.scalar
            def _(act):
                def copy_x(t, u):
                    act.wait_ge(x_turned, t + 1)
                    act.activation(XT3[:, u], PS[:, u, 0:C].rearrange("p (k m) -> p k m", k=2), ACT.Copy
                                   ).then_inc(xt_copied, 1)

                def relu(t, u):
                    act.wait_ge(h_turned, t + 1)
                    e = act.value_load(tile_e[0:1, ds(t, 1)], min_val=0, max_val=E - 1)
                    for j in (0, 1):
                        last = act.activation(HT3[:, u, j, :], PS[:, 4 + j // 2, (j % 2) * P:(j % 2 + 1) * P], ACT.Relu,
                                              bias=b1T[:, ds(e, 1), j])
                    last.then_inc(relu_act, 1)

                copy_x(0, 0)
                copy_x(1, 1)
                relu(0, 0)

                def step(t, u, i):
                    act.wait_ge(mm1_done, t + 0)
                    copy_x(t + 1, 1 - u)
                    wait_past(act, mm2_done, t - 1)
                    relu(t, u)
                odd_even(act, step)
                act.wait_ge(mm2_done, MT - 2)
                relu(MT - 1, 1)

            @block.vector
            def _(dve):
                def copy_h(t, u):
                    dve.wait_ge(mm1_done, t + 1)
                    nc.vector.tensor_copy(H3[:, u, :], PS[:, 2 + u, :]).then_inc(h_copied, 1)

                def relu(t, u):
                    dve.wait_ge(h_turned, t + 1)
                    e = dve.value_load(tile_e[0:1, ds(t, 1)], min_val=0, max_val=E - 1)
                    for j in (2, 3):
                        last = nc.vector.tensor_scalar(HT3[:, u, j, :], PS[:, 4 + j // 2, (j % 2) * P:(j % 2 + 1) * P],
                                                       b1T[:, ds(e, 1), j], 0.0, ALU.add, ALU.max)
                    last.then_inc(relu_dve, 1)

                def copy_o(t, u, half):
                    dve.wait_ge(mm2_done, t + 1)
                    wait_past(dve, o_sent[u], 16 * half)
                    nc.vector.tensor_copy(O3[:, u, :], PS[:, 6 + u, 0:C]).then_inc(o_copied, 1)

                copy_h(0, 0)
                relu(0, 0)

                def step(t, u, i):
                    wait_past(dve, h_turned, t - 1)
                    copy_h(t, u)
                    copy_o(t - 1, 1 - u, i if u == 1 else i - 1)
                    relu(t, u)
                odd_even(dve, step)
                dve.wait_ge(h_turned, MT - 2)
                copy_h(MT - 1, 1)
                copy_o(MT - 2, 0, MT // 2 - 1)
                relu(MT - 1, 1)
                copy_o(MT - 1, 1, MT // 2 - 1)

            @block.gpsimd
            def _(pool):
                for e in range(MIDDLE, E):
                    load_expert(pool, e, late_in)
                    pool.wait_ge(late_in, 32 * (e - MIDDLE + 1))
                    pool.sem_inc(experts_ready, 1)
                link = linker(pool, pool3)
                PER = 2 * 9 + 2
                with pool.Fori(0, NGT) as g:
                    link.rebase(g * PER)
                    tiles = ds(g * GT, GT)
                    for k in range(2):
                        link(nc.gpsimd.tensor_tensor(oh[:, k], iota16[:, :].unsqueeze(1).to_broadcast([P, GT, E]),
                                                     IDX[:, tiles, k:k + 1].to_broadcast([P, GT, E]), ALU.subtract))
                        pool.sem_inc(wait_mark, 1)
                        link(nc.gpsimd.tensor_scalar(oh[:, k], oh[:, k], 0.0, None, ALU.is_equal))
                        link(nc.gpsimd.tensor_tensor(prodq[:, :, :], oh[:, k],
                                                     dbase[:, :].unsqueeze(1).to_broadcast([P, GT, E]), ALU.mult))
                        for half in (8, 4, 2, 1):
                            link(nc.gpsimd.tensor_tensor(prodq[:, :, 0:half], prodq[:, :, 0:half],
                                                         prodq[:, :, half:2 * half], ALU.add))
                        link(nc.gpsimd.tensor_tensor(SLOT[:, tiles, k:k + 1], SLOT[:, tiles, k:k + 1],
                                                     prodq[:, :, 0:1], ALU.add))
                        link(nc.gpsimd.tensor_tensor(oh[:, k], oh[:, k],
                                                     WT[:, k, tiles].unsqueeze(2).to_broadcast([P, GT, E]), ALU.mult))
                    link(nc.gpsimd.tensor_tensor(GM[:, tiles, :], oh[:, 0], oh[:, 1], ALU.add))
                    link(nc.gpsimd.tensor_copy(SLOTI[:, tiles, :], SLOT[:, tiles, :]))
                    assert link.state[1] == PER, link.state

        affine_in = sem("affine_in")
        idx_copied = sem("idx_copied")
        picks_in = [sem("picks_in0"), sem("picks_in1")]
        picks_free = sem("picks_free")
        gm_copied = sem("gm_copied")
        gm_turned = sem("gm_turned")
        gmT_copied = sem("gmT_copied")
        xn4_ready = sem("xn4_ready")
        base_done = sem("base_done")
        base_read = sem("base_read")
        acc_step = sem("acc_step")
        var4 = sem("var4")
        sd4_ready = sem("sd4_ready")
        rs4_ready = sem("rs4_ready")
        norm4 = sem("norm4")
        y4_ready = sem("y4_ready")
        y4_free = sem("y4_free")
        fin_step = sem("fin_step")
        out_ready = sem("out_ready")
        out_sent = [sem("out_sent0"), sem("out_sent1")]

        def base_bank(u, j):
            return 2 + (j + u) % 6

        def bank_before(u, j):
            earlier = [d for d in range(1, GT + j + 1)
                       if base_bank(u if d <= j else 1 - u, (j - d) % GT) == base_bank(u, j)]
            return earlier[0]

        with nc.Block() as block:
            @block.sync
            def _(sp):
                sp.dma_start(gamma_bc, gamma.partition_broadcast(P)).then_inc(affine_in, 16)
                sp.dma_start(beta_bc, beta.partition_broadcast(P)).then_inc(affine_in, 16)

                def store(g, i, u, last):
                    sp.wait_ge(out_ready, g + 1)
                    full = GT - 1 if last else GT
                    sp.dma_start(out[ds(g * (GT * P), full * P), :].rearrange("(t p) c -> p t c", p=P),
                                 out4[:, u, 0:full]).then_inc(out_sent[u], 16)
                    if last:
                        sp.dma_start(out[(NT - 1) * P:N, :], out4[0:LAST, u, GT - 1, :]).then_inc(out_sent[u], 16)
                pairs(sp, store)
                sp.wait_ge(out_sent[0], 16 * (NGT // 2 + 2))
                sp.wait_ge(out_sent[1], 16 * (NGT // 2))

            @block.gpsimd
            def _(pool):
                def pick(g, i, u, last):
                    wait_past(pool, picks_free, g - 1)
                    nc.gpsimd.tensor_copy(gidx[u], SLOTI[:, ds(g * GT, GT), :].rearrange("p t k -> p (t k)")
                                          ).then_inc(idx_copied, 1)
                    pool.wait_ge(idx_copied, g + 1)
                    pool.sem_inc(wait_mark, 1)
                    for j in range(GT):
                        rows = LAST if last and j == GT - 1 else P
                        for k in range(2):
                            nc.gpsimd.indirect_dma_start(
                                out=picks[u][0:rows, j, k, :], out_offset=None, in_=ys[:, :],
                                in_offset=bass.IndirectOffsetOnAxis(ap=gidx[u][0:rows, 2 * j + k:2 * j + k + 1], axis=0)
                            ).then_inc(picks_in[u], 16)
                pairs(pool, pick)

            @block.scalar
            def _(act):
                def front(g, u):
                    wait_past(act, base_done, GT * (g - 1))
                    act.activation(gm_s[:, u], GM[:, ds(g * GT, GT), :], ACT.Copy).then_inc(gm_copied, 1)
                    for j in range(GT):
                        act.activation(xn4[:, u, j, :], XH[:, ds(g * GT + j, 1), :].rearrange("p o c -> p (o c)"),
                                       ACT.Identity, bias=nmr[:, ds(g * GT + j, 1)],
                                       scale=rstd[:, ds(g * GT + j, 1)]).then_inc(xn4_ready, 1)
                    act.wait_ge(gm_turned, g + 1)
                    act.activation(gmT[0:E, u, 0:4, :], PS[0:E, 0, :].rearrange("p (j m) -> p j m", m=P), ACT.Copy
                                   ).then_inc(gmT_copied, 1)
                    act.activation(gmT[0:E, u, 4:GT, :],
                                   PS[0:E, 1, 0:(GT - 4) * P].rearrange("p (j m) -> p j m", m=P), ACT.Copy
                                   ).then_inc(gmT_copied, 1)

                def back(g, u):
                    act.wait_ge(var4, g + 1)
                    act.activation(sd4[:, u, :], ve4[:, u, :], ACT.Sqrt).then_inc(sd4_ready, 1)
                    act.wait_ge(norm4, g + 1)
                    wait_past(act, y4_free, g - 1)
                    for j in range(GT):
                        act.activation(y4[:, u, j, :], acc4[:, u, j, :], ACT.Identity, bias=nm4[:, u, j:j + 1],
                                       scale=rs4[:, u, j:j + 1]).then_inc(y4_ready, 1)

                front(0, 0)
                front(1, 1)
                back(0, 0)
                front(2, 0)
                back(1, 1)
                with act.Fori(1, NGT // 2) as i:
                    front(2 * i + 1, 1)
                    back(2 * i, 0)
                    front(2 * i + 2, 0)
                    back(2 * i + 1, 1)
                back(NGT - 1, 0)

            @block.tensor
            def _(pe):
                def base(g, i, u, last):
                    pe.wait_ge(gm_copied, g + 1)
                    wait_past(pe, gmT_copied, 2 * g)
                    for j in range(GT):
                        ins = nc.tensor.transpose(PS[0:E, j // 4, (j % 4) * P:(j % 4 + 1) * P], gm_s[:, u, j, :],
                                                  ident[:, :])
                    ins.then_inc(gm_turned, 1)
                    pe.wait_ge(gmT_copied, 2 * g + 2)
                    for j in range(GT):
                        o = PS[:, base_bank(u, j), 0:C]
                        wait_past(pe, base_read, GT * g + (j + 1 - bank_before(u, j)))
                        nc.tensor.matmul(o, gmT[0:E, u, j, :], b2_sb[:, :], start=True, stop=False)
                        pe.wait_ge(xn4_ready, GT * g + (j + 1))
                        nc.tensor.matmul(o, ident[:, :], xn4[:, u, j, :], start=False, stop=True
                                         ).then_inc(base_done, 1)
                pairs(pe, base)

            @block.vector
            def _(dve):
                dve.wait_ge(affine_in, 32)

                def gather_sum(g, u, i):
                    dve.wait_ge(picks_in[u], (32 * GT) * (i + 1))
                    for j in range(GT):
                        dve.wait_ge(base_done, GT * g + (j + 1))
                        nc.vector.scalar_tensor_tensor(acc4[:, u, j, :], picks[u][:, j, 0, :],
                                                       WT[:, 0, ds(g * GT + j, 1)],
                                                       PS[:, base_bank(u, j), 0:C], ALU.mult, ALU.add
                                                       ).then_inc(base_read, 1)
                    dve.wait_ge(base_read, GT * g + GT)
                    for j in range(GT):
                        ins = nc.vector.scalar_tensor_tensor(acc4[:, u, j, :], picks[u][:, j, 1, :],
                                                             WT[:, 1, ds(g * GT + j, 1)],
                                                             acc4[:, u, j, :], ALU.mult, ALU.add)
                    ins.then_inc(picks_free, 1)
                    dve.wait_ge(picks_free, g + 1)
                    for j in range(GT):
                        ins = nc.vector.bn_stats(st4[:, j, :], acc4[:, u, j, :])
                    ins.then_inc(acc_step, 1)
                    dve.wait_ge(acc_step, 2 * g + 1)
                    dve.sem_inc(wait_mark, 1)
                    for j in range(GT):
                        ins = nc.vector.bn_aggr(mv4[:, u, j, :], st4[:, j, :])
                    ins.then_inc(acc_step, 1)
                    dve.wait_ge(acc_step, 2 * g + 2)
                    nc.vector.tensor_scalar(ve4[:, u, :], mv4[:, u, :, 1], EPS, None, ALU.add).then_inc(var4, 1)

                def scales(g, u):
                    dve.wait_ge(sd4_ready, g + 1)
                    nc.vector.reciprocal(rs4[:, u, :], sd4[:, u, :]).then_inc(rs4_ready, 1)
                    dve.wait_ge(rs4_ready, g + 1)
                    nc.vector.scalar_tensor_tensor(nm4[:, u, :], mv4[:, u, :, 0], -1.0, rs4[:, u, :],
                                                   ALU.mult, ALU.mult).then_inc(norm4, 1)

                def finish(g, u, i):
                    dve.wait_ge(y4_ready, GT * g + GT)
                    wait_past(dve, out_sent[u], 16 * i)
                    o = out4[:, u]
                    nc.vector.tensor_tensor(o, y4[:, u], gamma_bc.unsqueeze(1).to_broadcast([P, GT, C]),
                                            ALU.mult).then_inc(y4_free, 1)
                    dve.wait_ge(y4_free, g + 1)
                    nc.vector.tensor_tensor(o, o, XH[:, ds(g * GT, GT), :], ALU.add).then_inc(fin_step, 1)
                    dve.wait_ge(fin_step, g + 1)
                    nc.vector.tensor_tensor(o, o, beta_bc.unsqueeze(1).to_broadcast([P, GT, C]), ALU.add
                                            ).then_inc(out_ready, 1)

                gather_sum(0, 0, 0)
                scales(0, 0)

                def pair(i):
                    gather_sum(2 * i + 1, 1, i)
                    finish(2 * i, 0, i)
                    scales(2 * i + 1, 1)
                    gather_sum(2 * i + 2, 0, i + 1)
                    finish(2 * i + 1, 1, i)
                    scales(2 * i + 2, 0)
                pair(0)
                with dve.Fori(1, NGT // 2) as i:
                    pair(i)
                finish(NGT - 1, 0, NGT // 2)


_INS = ['x', 'src', 'dst', 'L0_gnn_W1', 'L0_gnn_b1', 'L0_gnn_W2', 'L0_gnn_b2', 'L0_ffn_gate_w', 'L0_ffn_gate_b',
        'L0_ffn_w1', 'L0_ffn_b1', 'L0_ffn_w2', 'L0_ffn_b2', 'L0_ffn_gamma', 'L0_ffn_beta']


def kernel(**inputs):
    import numpy as _np
    import concourse.bacc as _bacc
    from concourse import mybir as _mybir
    from concourse.bass_utils import run_bass_kernel_spmd as _run

    nc = _bacc.Bacc("TRN2", target_bir_lowering=False, num_devices=1)
    arrays, args = {}, []
    for name in _INS:
        a = _np.ascontiguousarray(inputs[name])
        arrays[f"in_{name}"] = a
        args.append(nc.dram_tensor(f"in_{name}", a.shape, _mybir.dt.from_np(a.dtype), kind="ExternalInput").ap())
    args.append(nc.dram_tensor("out_0", (N, C), _mybir.dt.float32, kind="ExternalOutput").ap())
    build(nc, *args)
    r = _run(nc, [arrays], core_ids=[0])
    return r.results[0]["out_0"]
```
